# Optimizing a Trainium2 kernel written in Bass

```python
import numpy as np
import jax
import jax.numpy as jnp

def _softmax(x, axis=-1):
    return jax.nn.softmax(x, axis=axis)
def _gelu(x):
    return jax.nn.gelu(x, approximate=True)
def _silu(x):
    return jax.nn.silu(x)
def _sigmoid(x):
    return jax.nn.sigmoid(x)
def _layernorm(x, axis=-1, eps=1e-5):
    m = jnp.mean(x, axis=axis, keepdims=True)
    v = jnp.var(x, axis=axis, keepdims=True)
    return (x - m) / jnp.sqrt(v + eps)
def _scatter_add(tgt, idx, src, axis=0):
    return tgt.at[idx].add(src)
def _segment_sum(src, seg, n):
    return jax.ops.segment_sum(src, seg, n)

kernel_name = 'mk_conv_seq_d2_conv_nchw128_f02456'

def setup_inputs(seed: int = 0):
    np.random.seed(seed)
    _w = jnp.asarray
    def _rec_inputs():
        import jax
        import jax.numpy as jnp
        _gk = jax.random.key(seed)
        x = -0.0003929 + 0.9999 * jax.random.normal(jax.random.fold_in(_gk, 1), (8, 128, 128, 128), jnp.float32)
        return x
    x = _rec_inputs()
    def _L0_conv_setup():
        import jax, jax.numpy as jnp
        import numpy as np
        BN_EPS = 1e-05
        EPS = 1e-06

        def _conv(x, w, pad, dil):
            return jax.lax.conv_general_dilated(x, w, window_strides=(1, 1), padding=[(pad, pad), (pad, pad)], rhs_dilation=(dil, dil), dimension_numbers=('NCHW', 'OIHW', 'NCHW'))

        def _bn_relu(x, s, b, m, v):
            inv = (s / jnp.sqrt(v + BN_EPS))[None, :, None, None]
            return jax.nn.relu((x - m[None, :, None, None]) * inv + b[None, :, None, None])

        def _l2n(x):
            return x / jnp.linalg.norm(x, axis=1, keepdims=True)

        def _forward(x, w1, w2, w3, w4, bn_scale, bn_bias, bn_mean, bn_var, wq, bq, wk, bk, wv, bv, gamma):
            B, C, H, W = x.shape
            N = H * W
            specs = [(w1, 0, 1), (w2, 6, 6), (w3, 12, 12), (w4, 18, 18)]
            branches = [_bn_relu(_conv(x, w, p, d), bn_scale[i], bn_bias[i], bn_mean[i], bn_var[i]) for i, (w, p, d) in enumerate(specs)]
            x_q = jnp.concatenate(branches, axis=1)
            Q = (jnp.einsum('oi,bihw->bohw', wq[:, :, 0, 0], x_q) + bq[None, :, None, None]).reshape(B, -1, N)
            K = (jnp.einsum('oi,bihw->bohw', wk[:, :, 0, 0], x) + bk[None, :, None, None]).reshape(B, -1, N)
            V = (jnp.einsum('oi,bihw->bohw', wv[:, :, 0, 0], x) + bv[None, :, None, None]).reshape(B, -1, N)
            Qn = _l2n(Q).transpose(0, 2, 1)
            Kn = _l2n(K)
            tailor = 1.0 / (N + jnp.einsum('bnm,bm->bn', Qn, Kn.sum(-1) + EPS))
            vsum = V.sum(-1)[:, :, None]
            mat = jnp.einsum('bmn,bcn->bmc', Kn, V)
            msum = vsum + jnp.einsum('bnm,bmc->bcn', Qn, mat)
            out = (msum * tailor[:, None, :]).reshape(B, C, H, W)
            return gamma * out
        key = jax.random.key(seed)
        ks = jax.random.split(key, 12)
        B, C, H, W = (8, 128, 128, 128)
        M = 16
        d = {'x': jax.random.normal(ks[0], (B, C, H, W), jnp.float32), 'w1': jax.random.normal(ks[1], (32, 128, 1, 1), jnp.float32) * 0.05, 'w2': jax.random.normal(ks[2], (32, 128, 3, 3), jnp.float32) * 0.05, 'w3': jax.random.normal(ks[3], (32, 128, 3, 3), jnp.float32) * 0.05, 'w4': jax.random.normal(ks[4], (32, 128, 3, 3), jnp.float32) * 0.05, 'bn_scale': jnp.ones((4, 32), jnp.float32), 'bn_bias': jnp.zeros((4, 32), jnp.float32), 'bn_mean': jnp.zeros((4, 32), jnp.float32), 'bn_var': jnp.ones((4, 32), jnp.float32), 'wq': jax.random.normal(ks[5], (M, 128, 1, 1), jnp.float32) * 0.05, 'bq': jax.random.normal(ks[6], (M,), jnp.float32) * 0.05, 'wk': jax.random.normal(ks[7], (M, 128, 1, 1), jnp.float32) * 0.05, 'bk': jax.random.normal(ks[8], (M,), jnp.float32) * 0.05, 'wv': jax.random.normal(ks[9], (C, 128, 1, 1), jnp.float32) * 0.05, 'bv': jax.random.normal(ks[10], (C,), jnp.float32) * 0.05, 'gamma': jax.random.uniform(ks[11], (1,), jnp.float32)}
        return d
    _L0_conv_all = _L0_conv_setup()
    _L0_conv_in = {k: v for k, v in _L0_conv_all.items() if k in ('w1', 'w2', 'w3', 'w4', 'bn_scale', 'bn_bias', 'bn_mean', 'bn_var', 'wq', 'bq', 'wk', 'bk', 'wv', 'bv', 'gamma', )}
    del _L0_conv_all

    def _L1_conv_setup():
        import jax, jax.numpy as jnp
        import numpy as np
        D_MODEL = 128
        D_STATE = 16
        D_CONV = 2
        EXPAND = 2
        D_INNER = EXPAND * D_MODEL
        DT_RANK = (D_MODEL + 15) // 16
        GROUPS = 4
        EPS = 1e-05

        def _causal_conv_k2(x, w, b):
            xp = jnp.pad(x, ((0, 0), (1, 0), (0, 0)))
            return xp[:, :-1] * w[:, 0] + xp[:, 1:] * w[:, 1] + b

        def _selective_scan(xc, dt, Bmat, Cmat, A, D):

            def step(h, inp):
                dt_t, B_t, C_t, x_t = inp
                dA = jnp.exp(dt_t[..., None] * A)
                dBx = dt_t[..., None] * B_t[:, None, :] * x_t[..., None]
                h = dA * h + dBx
                y = jnp.einsum('bdn,bn->bd', h, C_t)
                return (h, y)
            B_, L, Din = xc.shape
            h0 = jnp.zeros((B_, Din, A.shape[1]), dtype=xc.dtype)
            xs = (jnp.swapaxes(dt, 0, 1), jnp.swapaxes(Bmat, 0, 1), jnp.swapaxes(Cmat, 0, 1), jnp.swapaxes(xc, 0, 1))
            _, ys = jax.lax.scan(step, h0, xs)
            return jnp.swapaxes(ys, 0, 1) + xc * D

        def _mamba(x, W_in, conv_w, conv_b, W_x, W_dt, b_dt, A_log, D, W_out):
            xz = x @ W_in
            xh, z = jnp.split(xz, 2, axis=-1)
            xh = jax.nn.silu(_causal_conv_k2(xh, conv_w, conv_b))
            x_dbl = xh @ W_x
            dt_low = x_dbl[..., :DT_RANK]
            Bmat = x_dbl[..., DT_RANK:DT_RANK + D_STATE]
            Cmat = x_dbl[..., DT_RANK + D_STATE:]
            dt = jax.nn.softplus(dt_low @ W_dt + b_dt)
            A = -jnp.exp(A_log)
            y = _selective_scan(xh, dt, Bmat, Cmat, A, D)
            y = y * jax.nn.silu(z)
            return y @ W_out

        def _group_norm(x, gamma, beta):
            B_, C, H, W = x.shape
            xr = x.reshape(B_, GROUPS, -1)
            mean = xr.mean(-1, keepdims=True)
            var = xr.var(-1, keepdims=True)
            xn = ((xr - mean) * jax.lax.rsqrt(var + EPS)).reshape(B_, C, H, W)
            return xn * gamma[:, None, None] + beta[:, None, None]
        key = jax.random.key(seed)
        ks = jax.random.split(key, 12)
        s = lambda k, shape, sc=0.02: jax.random.normal(k, shape, dtype=jnp.float32) * sc
        inp = {'x_hsi': jax.random.normal(ks[0], (8, D_MODEL, 64, 64), dtype=jnp.float32), 'W_in': s(ks[1], (D_MODEL, 2 * D_INNER)), 'conv_w': s(ks[2], (D_INNER, D_CONV), 0.5), 'conv_b': s(ks[3], (D_INNER,), 0.1), 'W_x': s(ks[4], (D_INNER, DT_RANK + 2 * D_STATE)), 'W_dt': s(ks[5], (DT_RANK, D_INNER), 0.1), 'b_dt': s(ks[6], (D_INNER,), 0.1), 'A_log': jnp.log(jnp.broadcast_to(jnp.arange(1, D_STATE + 1, dtype=jnp.float32), (D_INNER, D_STATE))), 'D': jnp.ones((D_INNER,), dtype=jnp.float32), 'W_out': s(ks[7], (D_INNER, D_MODEL)), 'gn_gamma': jnp.ones((D_MODEL,), dtype=jnp.float32), 'gn_beta': jnp.zeros((D_MODEL,), dtype=jnp.float32)}
        return inp
    _L1_conv_all = _L1_conv_setup()
    _L1_conv_in = {k: v for k, v in _L1_conv_all.items() if k in ('W_in', 'conv_w', 'conv_b', 'W_x', 'W_dt', 'b_dt', 'A_log', 'D', 'W_out', 'gn_gamma', 'gn_beta', )}
    del _L1_conv_all

    return {
        "x": x,
        "L0_conv_w1": _L0_conv_in["w1"],
        "L0_conv_w2": _L0_conv_in["w2"],
        "L0_conv_w3": _L0_conv_in["w3"],
        "L0_conv_w4": _L0_conv_in["w4"],
        "L0_conv_bn_scale": _L0_conv_in["bn_scale"],
        "L0_conv_bn_bias": _L0_conv_in["bn_bias"],
        "L0_conv_bn_mean": _L0_conv_in["bn_mean"],
        "L0_conv_bn_var": _L0_conv_in["bn_var"],
        "L0_conv_wq": _L0_conv_in["wq"],
        "L0_conv_bq": _L0_conv_in["bq"],
        "L0_conv_wk": _L0_conv_in["wk"],
        "L0_conv_bk": _L0_conv_in["bk"],
        "L0_conv_wv": _L0_conv_in["wv"],
        "L0_conv_bv": _L0_conv_in["bv"],
        "L0_conv_gamma": _L0_conv_in["gamma"],
        "L1_conv_W_in": _L1_conv_in["W_in"],
        "L1_conv_conv_w": _L1_conv_in["conv_w"],
        "L1_conv_conv_b": _L1_conv_in["conv_b"],
        "L1_conv_W_x": _L1_conv_in["W_x"],
        "L1_conv_W_dt": _L1_conv_in["W_dt"],
        "L1_conv_b_dt": _L1_conv_in["b_dt"],
        "L1_conv_A_log": _L1_conv_in["A_log"],
        "L1_conv_D": _L1_conv_in["D"],
        "L1_conv_W_out": _L1_conv_in["W_out"],
        "L1_conv_gn_gamma": _L1_conv_in["gn_gamma"],
        "L1_conv_gn_beta": _L1_conv_in["gn_beta"],
    }

def reference(x, L0_conv_w1, L0_conv_w2, L0_conv_w3, L0_conv_w4, L0_conv_bn_scale, L0_conv_bn_bias, L0_conv_bn_mean, L0_conv_bn_var, L0_conv_wq, L0_conv_bq, L0_conv_wk, L0_conv_bk, L0_conv_wv, L0_conv_bv, L0_conv_gamma, L1_conv_W_in, L1_conv_conv_w, L1_conv_conv_b, L1_conv_W_x, L1_conv_W_dt, L1_conv_b_dt, L1_conv_A_log, L1_conv_D, L1_conv_W_out, L1_conv_gn_gamma, L1_conv_gn_beta):
    import jax
    import jax.numpy as jnp
    def _L0_conv_ref(x, w1, w2, w3, w4, bn_scale, bn_bias, bn_mean, bn_var, wq, bq, wk, bk, wv, bv, gamma):
        import jax, jax.numpy as jnp
        import numpy as np
        BN_EPS = 1e-05
        EPS = 1e-06

        def _conv(x, w, pad, dil):
            return jax.lax.conv_general_dilated(x, w, window_strides=(1, 1), padding=[(pad, pad), (pad, pad)], rhs_dilation=(dil, dil), dimension_numbers=('NCHW', 'OIHW', 'NCHW'))

        def _bn_relu(x, s, b, m, v):
            inv = (s / jnp.sqrt(v + BN_EPS))[None, :, None, None]
            return jax.nn.relu((x - m[None, :, None, None]) * inv + b[None, :, None, None])

        def _l2n(x):
            return x / jnp.linalg.norm(x, axis=1, keepdims=True)

        def _forward(x, w1, w2, w3, w4, bn_scale, bn_bias, bn_mean, bn_var, wq, bq, wk, bk, wv, bv, gamma):
            B, C, H, W = x.shape
            N = H * W
            specs = [(w1, 0, 1), (w2, 6, 6), (w3, 12, 12), (w4, 18, 18)]
            branches = [_bn_relu(_conv(x, w, p, d), bn_scale[i], bn_bias[i], bn_mean[i], bn_var[i]) for i, (w, p, d) in enumerate(specs)]
            x_q = jnp.concatenate(branches, axis=1)
            Q = (jnp.einsum('oi,bihw->bohw', wq[:, :, 0, 0], x_q) + bq[None, :, None, None]).reshape(B, -1, N)
            K = (jnp.einsum('oi,bihw->bohw', wk[:, :, 0, 0], x) + bk[None, :, None, None]).reshape(B, -1, N)
            V = (jnp.einsum('oi,bihw->bohw', wv[:, :, 0, 0], x) + bv[None, :, None, None]).reshape(B, -1, N)
            Qn = _l2n(Q).transpose(0, 2, 1)
            Kn = _l2n(K)
            tailor = 1.0 / (N + jnp.einsum('bnm,bm->bn', Qn, Kn.sum(-1) + EPS))
            vsum = V.sum(-1)[:, :, None]
            mat = jnp.einsum('bmn,bcn->bmc', Kn, V)
            msum = vsum + jnp.einsum('bnm,bmc->bcn', Qn, mat)
            out = (msum * tailor[:, None, :]).reshape(B, C, H, W)
            return gamma * out
        return _forward(x, w1, w2, w3, w4, bn_scale, bn_bias, bn_mean, bn_var, wq, bq, wk, bk, wv, bv, gamma)

    def _L1_conv_ref(x_hsi, W_in, conv_w, conv_b, W_x, W_dt, b_dt, A_log, D, W_out, gn_gamma, gn_beta):
        import jax, jax.numpy as jnp
        import numpy as np
        D_MODEL = 128
        D_STATE = 16
        D_CONV = 2
        EXPAND = 2
        D_INNER = EXPAND * D_MODEL
        DT_RANK = (D_MODEL + 15) // 16
        GROUPS = 4
        EPS = 1e-05

        def _causal_conv_k2(x, w, b):
            xp = jnp.pad(x, ((0, 0), (1, 0), (0, 0)))
            return xp[:, :-1] * w[:, 0] + xp[:, 1:] * w[:, 1] + b

        def _selective_scan(xc, dt, Bmat, Cmat, A, D):

            def step(h, inp):
                dt_t, B_t, C_t, x_t = inp
                dA = jnp.exp(dt_t[..., None] * A)
                dBx = dt_t[..., None] * B_t[:, None, :] * x_t[..., None]
                h = dA * h + dBx
                y = jnp.einsum('bdn,bn->bd', h, C_t)
                return (h, y)
            B_, L, Din = xc.shape
            h0 = jnp.zeros((B_, Din, A.shape[1]), dtype=xc.dtype)
            xs = (jnp.swapaxes(dt, 0, 1), jnp.swapaxes(Bmat, 0, 1), jnp.swapaxes(Cmat, 0, 1), jnp.swapaxes(xc, 0, 1))
            _, ys = jax.lax.scan(step, h0, xs)
            return jnp.swapaxes(ys, 0, 1) + xc * D

        def _mamba(x, W_in, conv_w, conv_b, W_x, W_dt, b_dt, A_log, D, W_out):
            xz = x @ W_in
            xh, z = jnp.split(xz, 2, axis=-1)
            xh = jax.nn.silu(_causal_conv_k2(xh, conv_w, conv_b))
            x_dbl = xh @ W_x
            dt_low = x_dbl[..., :DT_RANK]
            Bmat = x_dbl[..., DT_RANK:DT_RANK + D_STATE]
            Cmat = x_dbl[..., DT_RANK + D_STATE:]
            dt = jax.nn.softplus(dt_low @ W_dt + b_dt)
            A = -jnp.exp(A_log)
            y = _selective_scan(xh, dt, Bmat, Cmat, A, D)
            y = y * jax.nn.silu(z)
            return y @ W_out

        def _group_norm(x, gamma, beta):
            B_, C, H, W = x.shape
            xr = x.reshape(B_, GROUPS, -1)
            mean = xr.mean(-1, keepdims=True)
            var = xr.var(-1, keepdims=True)
            xn = ((xr - mean) * jax.lax.rsqrt(var + EPS)).reshape(B_, C, H, W)
            return xn * gamma[:, None, None] + beta[:, None, None]
        B_, C, H, W = x_hsi.shape
        x = jnp.transpose(x_hsi, (0, 2, 3, 1)).reshape(B_, H * W, C)
        x = _mamba(x, W_in, conv_w, conv_b, W_x, W_dt, b_dt, A_log, D, W_out)
        x = jnp.transpose(x.reshape(B_, H, W, C), (0, 3, 1, 2))
        x = jax.nn.silu(_group_norm(x, gn_gamma, gn_beta))
        return x + x_hsi

    def _gn(v, G=32, eps=1e-5):
        B_, C_, H_, W_ = v.shape
        g = v.reshape(B_, G, C_ // G, H_, W_)
        m = jnp.mean(g, axis=(2, 3, 4), keepdims=True)
        s = jnp.var(g, axis=(2, 3, 4), keepdims=True)
        return ((g - m) / jnp.sqrt(s + eps)).reshape(v.shape)

    def _ln_c(v, eps=1e-6):
        m = jnp.mean(v, axis=1, keepdims=True)
        s = jnp.var(v, axis=1, keepdims=True)
        return (v - m) / jnp.sqrt(s + eps)

    def _ln_t(v, eps=1e-5):
        m = jnp.mean(v, axis=-1, keepdims=True)
        s = jnp.var(v, axis=-1, keepdims=True)
        return (v - m) / jnp.sqrt(s + eps)

    def _to_tokens(v):
        B_, C_, H_, W_ = v.shape
        return v.reshape(B_, C_, H_ * W_).transpose(0, 2, 1)
    def _from_tokens(t, like):
        B_, C_, H_, W_ = like.shape
        return t.transpose(0, 2, 1).reshape(B_, C_, H_, W_)

    x = _L0_conv_ref(x, L0_conv_w1, L0_conv_w2, L0_conv_w3, L0_conv_w4, L0_conv_bn_scale, L0_conv_bn_bias, L0_conv_bn_mean, L0_conv_bn_var, L0_conv_wq, L0_conv_bq, L0_conv_wk, L0_conv_bk, L0_conv_wv, L0_conv_bv, L0_conv_gamma)
    x = _L1_conv_ref(x, L1_conv_W_in, L1_conv_conv_w, L1_conv_conv_b, L1_conv_W_x, L1_conv_W_dt, L1_conv_b_dt, L1_conv_A_log, L1_conv_D, L1_conv_W_out, L1_conv_gn_gamma, L1_conv_gn_beta)
    return x


_drawn_inputs = setup_inputs


def setup_inputs(seed=0):
    import zlib

    import numpy as np

    out = dict(_drawn_inputs(seed))
    spreads = {'L0_conv_bn_scale': (1.0, 0.6),
     'L0_conv_bn_bias': (0.0, 0.8),
     'L0_conv_bn_mean': (0.0, 0.8),
     'L0_conv_bn_var': (1.0, 0.6),
     'L1_conv_D': (1.0, 0.6),
     'L1_conv_gn_gamma': (1.0, 0.2),
     'L1_conv_gn_beta': (0.0, 0.1)}
    factors = {'L0_conv_w1': 2.771,
     'L0_conv_bq': 5.822,
     'L0_conv_bk': 28.237,
     'L1_conv_conv_w': 4.745,
     'L1_conv_W_x': 44.148,
     'L1_conv_W_dt': 64.0,
     'L1_conv_b_dt': 64.0,
     'L1_conv_A_log': 64.0}
    for name, (base, spread) in spreads.items():
        noise = np.random.default_rng([zlib.crc32(name.encode()), seed]).standard_normal(out[name].shape)
        drawn = base * np.exp(spread * noise) if base else spread * noise
        out[name] = jnp.asarray(drawn.astype(out[name].dtype))
    for name, factor in factors.items():
        out[name] = (out[name] * factor).astype(out[name].dtype)
    return out
```

```python
from contextlib import ExitStack

import concourse.bass as bass
from concourse import mybir

F32 = mybir.dt.float32
BF16 = mybir.dt.bfloat16
ALU = mybir.AluOpType
ACT = mybir.ActivationFunctionType
AX_X = mybir.AxisListType.X

B, C, H, W = 8, 128, 128, 128
N = H * W
M = 16
CH = 512
ROWS = CH // W
NCH = N // CH
SUB = CH // 128
PAD = 18
WP = W + 2 * PAD
BR = 32
DIL = (6, 12, 18)
TAPS = [(dy, dx) for dy in (-1, 0, 1) for dx in (-1, 0, 1) if (dy, dx) != (0, 0)]
KU = M + 1
K2 = 32 + KU
DI = 256
S = 16
R = 8
SLOTS = NCH + 1
LAYER0_EPS, BN_EPS, GN_EPS = 1e-6, 1e-5, 1e-5
GROUP = 32
TINY = 1e-30
LOG_MIN = 2.0 ** -24
A_LOG_MAX = 81.5
PIECE = 8
PIECES = H // PIECE
HC = 4
CB = 2048
NCB = N // CB


def phase_a(nc, t, uq, mat_dram):
    with ExitStack() as ctx:
        def sb(name, shape, dt=F32):
            return ctx.enter_context(nc.sbuf_tensor(name, shape, dt))

        def ps(name, shape):
            return ctx.enter_context(nc.psum_tensor(name, shape, F32))

        def sem(name):
            return ctx.enter_context(nc.semaphore(name))

        image = sb("image", [C, WP, WP])
        w_center = sb("w_center", [C, 4 * BR])
        w_taps = sb("w_taps", [C, 3, 8, BR])
        w_kv = sb("w_kv", [C, M + C])
        w_q = sb("w_q", [C, M])
        b_kv = sb("b_kv", [128, M + C])
        b_q = sb("b_q", [M, 1])
        bn = sb("bn", [C, 4])
        bn_std = sb("bn_std", [C, 1])
        bn_inv = sb("bn_inv", [C, 1])
        bn_mi = sb("bn_mi", [C, 1])
        bn_shift = sb("bn_shift", [C, 1])
        bn_eps = sb("bn_eps", [C, 1])
        ones_m = sb("ones_m", [M, 64])
        zero_chunk = sb("zero_chunk", [KU, CH])
        x_q = sb("x_q", [C, CH])
        q_sb = sb("q_sb", [M, 2, CH])
        s_sb = sb("s_sb", [65, 2, CH])
        q_sq = sb("q_sq", [M, CH])
        k_sb = sb("k_sb", [128, SUB, M])
        k_sq = sb("k_sq", [128, SUB, M])
        k_n2 = sb("k_n2", [128, SUB])
        k_nrm = sb("k_nrm", [128, SUB])
        k_inv = sb("k_inv", [128, SUB])
        kn1 = sb("kn1", [128, 2, SUB, KU])
        v1 = sb("v1", [128, 2, SUB, C + 1])
        mat = sb("mat", [KU, C + 1])

        conv_ps = ps("conv_ps", [128, 2, CH])
        kv_ps = ps("kv_ps", [128, 2, 2, CH])
        qs_ps = ps("qs_ps", [128, CH])
        mat_ps = ps("mat_ps", [128, CH])

        weights = sem("weights")
        cleared = sem("cleared")
        set_up = sem("set_up")
        bn_root = sem("bn_root")
        pads_stored = sem("pads_stored")
        x_loaded = sem("x_loaded")
        conv_done = sem("conv_done")
        bn_done = sem("bn_done")
        kv_done = sem("kv_done")
        k_done = sem("k_done")
        ksq_done = sem("ksq_done")
        kn2_done = sem("kn2_done")
        v_done = sem("v_done")
        knrm_done = sem("knrm_done")
        kinv_done = sem("kinv_done")
        kn_done = sem("kn_done")
        q_mm = sem("q_mm")
        q_done = sem("q_done")
        sq_done = sem("sq_done")
        s2_mm = sem("s2_mm")
        s_done = sem("s_done")
        u_stored = [sem(f"u_stored{p}") for p in range(2)]
        mat_mm = sem("mat_mm")
        mat_done = sem("mat_done")
        mat_zero = sem("mat_zero")
        mat_stored = sem("mat_stored")

        block = ctx.enter_context(nc.Block())

        @block.sync
        def _(sp):
            for dst, src in ((w_center[:], t["w_center"]), (w_taps[:], t["w_taps"]), (w_kv[:], t["w_kv"]),
                             (w_q[:], t["w_q"]), (b_kv[:], t["b_kv"].partition_broadcast(128)),
                             (b_q[:], t["b_q"]), (bn[:], t["bn"])):
                sp.dma_start(dst, src).then_inc(weights, 16)
            sp.wait_ge(cleared, 5)
            for i in range(4):
                rows = slice(i * 32, i * 32 + 32)
                sp.dma_start(image[:, PAD + 32 * i:PAD + 32 * i + 32, PAD:PAD + W],
                             t["x"][0, :, rows, :]).then_inc(x_loaded, 16)
            for b in range(B + 1):
                sp.dma_start(uq[:, b * SLOTS * CH:b * SLOTS * CH + CH], zero_chunk[:]).then_inc(pads_stored, 16)

            with sp.Fori(1, B) as b:
                with sp.Fori(0, PIECES - 3) as j:
                    sp.wait_ge(conv_done, (b - 1) * NCH + 2 * j + 7)
                    sp.dma_start(image[:, bass.ds(j * PIECE + PAD, PIECE), PAD:PAD + W],
                                 t["x"][bass.ds(b, 1), :, bass.ds(j * PIECE, PIECE), :]
                                 .rearrange("o c h w -> (o c) h w")).then_inc(x_loaded, 16)
                sp.wait_ge(conv_done, b * NCH)
                rest = (PIECES - 3) * PIECE
                sp.dma_start(image[:, PAD + rest:PAD + H, PAD:PAD + W],
                             t["x"][bass.ds(b, 1), :, rest:H, :]
                             .rearrange("o c h w -> (o c) h w")).then_inc(x_loaded, 16)
            sp.wait_ge(pads_stored, 16 * (B + 1))
            sp.wait_ge(x_loaded, 16 * (4 + (B - 1) * (PIECES - 2)))

        def loaded(eng, b):
            eng.wait_ge(x_loaded, 16 * 4 + b * (16 * (PIECES - 2)))

        @block.gpsimd
        def _(pool):
            pool.memset(image[:], 0.0).then_inc(cleared, 1)
            pool.memset(zero_chunk[:], 0.0).then_inc(cleared, 1)
            pool.memset(ones_m[:], 1.0).then_inc(cleared, 1)
            pool.memset(kn1[:], 1.0).then_inc(cleared, 1)
            pool.memset(v1[:], 1.0).then_inc(cleared, 1)
            for p in range(2):
                pool.sem_inc(u_stored[p], 32)
            pool.sem_inc(mat_stored, 16)

        @block.scalar
        def _(act):
            act.wait_ge(weights, 16 * 7)
            act.wait_ge(set_up, 1)
            nc.scalar.activation(bn_std[:], bn[:, 3:4], ACT.Sqrt, bias=bn_eps[:]).then_inc(bn_root, 1)
            act.sem_inc(bn_done, 2)
            act.sem_inc(s_done, 1)
            act.wait_ge(set_up, 5)

            def relu(b, r, p):
                act.wait_ge(conv_done, b * NCH + r + 1)
                act.wait_ge(q_mm, b * NCH + r + 1)
                nc.scalar.activation(x_q[:], conv_ps[:, p], ACT.Relu, bias=bn_shift[:], scale=bn_inv[:]
                                     ).then_inc(bn_done, 1)

            def norms(b, r, p):
                k = b * NCH + r
                act.wait_ge(kn2_done, k + 1)
                act.wait_ge(kinv_done, k + 1)
                nc.scalar.activation(k_nrm[:], k_n2[:], ACT.Sqrt).then_inc(knrm_done, 1)

            def query(b, j, p):
                r = 2 * j + p
                k = b * NCH + r
                act.wait_ge(q_mm, k + 2)
                act.wait_ge(u_stored[p], 32 * (b * (NCH // 2) + j + 1))
                nc.scalar.activation(q_sb[:, p], qs_ps[0:M, :], ACT.Identity, bias=b_q[:]).then_inc(q_done, 1)
                act.wait_ge(s2_mm, k + 1)
                nc.scalar.activation(q_sq[:], qs_ps[0:M, :], ACT.Square, bias=b_q[:]).then_inc(sq_done, 1)
                act.wait_ge(s2_mm, k + 2)
                nc.scalar.activation(s_sb[64:65, p], qs_ps[64:65, :], ACT.Sqrt).then_inc(s_done, 1)
                act.wait_ge(q_done, k + 1)
                act.wait_ge(s_done, k + 2)
                c0 = (b * SLOTS + r + 1) * CH
                act.dma_start(uq[0:M, bass.ds(c0, CH)], q_sb[:, p]).then_inc(u_stored[p], 16)
                act.dma_start(uq[M:KU, bass.ds(c0, CH)], s_sb[64:65, p]).then_inc(u_stored[p], 16)

            with act.Fori(0, B) as b:
                with act.Fori(0, NCH // 2) as j:
                    for p in range(2):
                        relu(b, 2 * j + p, p)
                        norms(b, 2 * j + p, p)
                        query(b, j, p)
                act.wait_ge(mat_done, (b + 1) * NCH + 1)
                act.dma_start(mat_dram[bass.ds(b, 1), :, :].rearrange("o k c -> (o k) c"), mat[:]
                              ).then_inc(mat_stored, 16)
            for p in range(2):
                act.wait_ge(u_stored[p], 32 * (B * NCH // 2 + 1))
            act.wait_ge(mat_stored, 16 * (B + 1))

        @block.tensor
        def _(pe):
            pe.wait_ge(weights, 16 * 7)
            pe.wait_ge(cleared, 5)
            pe.sem_inc(q_mm, 1)
            pe.sem_inc(s2_mm, 1)

            def kv(b, r, p):
                k = b * NCH + r
                pe.wait_ge(v_done, k + 1)
                for j in range(SUB):
                    last = nc.tensor.matmul(kv_ps[:, p, j // 2, (j % 2) * (M + C):(j % 2 + 1) * (M + C)],
                                            image[:, PAD + ROWS * r + j, PAD:PAD + W], w_kv[:], start=True, stop=True)
                last.then_inc(kv_done, 1)

            def conv(b, r, p):
                k = b * NCH + r
                pe.wait_ge(bn_done, k + 1)
                y0 = r * ROWS + PAD
                nc.tensor.matmul(conv_ps[:, p], w_center[:], image[:, y0:y0 + ROWS, PAD:PAD + W],
                                 start=True, stop=False, skip_group_check=True)
                steps = [(n, i) for n, (dy, _) in enumerate(TAPS) for i, d in enumerate(DIL)
                         if -ROWS < r * ROWS + dy * d < H]
                for n, i in steps:
                    y1, x1 = y0 + TAPS[n][0] * DIL[i], PAD + TAPS[n][1] * DIL[i]
                    last = nc.tensor.matmul(conv_ps[BR * (i + 1):BR * (i + 2), p], w_taps[:, i, n, :],
                                            image[:, y1:y1 + ROWS, x1:x1 + W],
                                            start=False, stop=(n == 7), skip_group_check=True)
                last.then_inc(conv_done, 1)

            def query(b, r, p):
                k = b * NCH + r
                pe.wait_ge(bn_done, k + 3)
                pe.wait_ge(s_done, k + 1)
                nc.tensor.matmul(qs_ps[0:M, :], w_q[:], x_q[:], start=True, stop=True).then_inc(q_mm, 1)

            def query_norm(b, r, p):
                k = b * NCH + r
                pe.wait_ge(sq_done, k + 1)
                nc.tensor.matmul(qs_ps[64:128, :], ones_m[:], q_sq[:], start=True, stop=True).then_inc(s2_mm, 1)

            def outer(b, r, p):
                k = b * NCH + r
                pe.wait_ge(kn_done, k + 2)
                pe.wait_ge(mat_done, k + 1)
                for j in range(SUB):
                    last = nc.tensor.matmul(mat_ps[0:KU, 0:C + 1], kn1[:, p, j, :], v1[:, p, j, :],
                                            start=(j == 0), stop=(j == SUB - 1))
                last.then_inc(mat_mm, 1)

            with pe.Fori(0, B) as b:
                loaded(pe, b)
                for r in range(NCH + 1):
                    p = r % 2
                    if r < NCH:
                        kv(b, r, p)
                    if r > 0:
                        query(b, r - 1, 1 - p)
                    if r < NCH:
                        conv(b, r, p)
                    if r > 0:
                        query_norm(b, r - 1, 1 - p)
                        outer(b, r - 1, 1 - p)

        @block.vector
        def _(dve):
            nc.vector.memset(bn_eps[:], BN_EPS).then_inc(set_up, 1)
            dve.wait_ge(bn_root, 1)
            nc.vector.reciprocal(bn_mi[:], bn_std[:]).then_inc(set_up, 1)
            dve.wait_ge(set_up, 2)
            nc.vector.tensor_tensor(bn_inv[:], bn_mi[:], bn[:, 0:1], ALU.mult).then_inc(set_up, 1)
            dve.wait_ge(set_up, 3)
            nc.vector.tensor_tensor(bn_mi[:], bn[:, 2:3], bn_inv[:], ALU.mult).then_inc(set_up, 1)
            dve.wait_ge(set_up, 4)
            nc.vector.tensor_tensor(bn_shift[:], bn[:, 1:2], bn_mi[:], ALU.subtract).then_inc(set_up, 1)
            dve.wait_ge(cleared, 5)
            dve.sem_inc(v_done, 2)
            dve.sem_inc(kinv_done, 1)
            dve.sem_inc(mat_done, 1)

            def keys(b, r, p):
                k = b * NCH + r
                dve.wait_ge(kv_done, k + 1)
                kv = kv_ps[:, p, :, 0:2 * (M + C)].rearrange("t a (j e) -> t a j e", j=2)
                dve.wait_ge(kn_done, k + 1)
                nc.vector.tensor_tensor(k_sb[:].rearrange("t (a j) m -> t a j m", a=2), kv[:, :, :, 0:M],
                                        b_kv[:, 0:M].unsqueeze(1).unsqueeze(1).broadcast_to([128, 2, 2, M]),
                                        ALU.add).then_inc(k_done, 1)
                dve.wait_ge(mat_mm, k + 1)
                nc.vector.tensor_tensor(v1[:, p, :, 0:C].rearrange("t (a j) c -> t a j c", a=2), kv[:, :, :, M:M + C],
                                        b_kv[:, M:M + C].unsqueeze(1).unsqueeze(1).broadcast_to([128, 2, 2, C]),
                                        ALU.add).then_inc(v_done, 1)
                dve.wait_ge(k_done, k + 1)
                nc.vector.tensor_tensor(k_sq[:], k_sb[:], k_sb[:], ALU.mult).then_inc(ksq_done, 1)
                dve.wait_ge(ksq_done, k + 1)
                dve.wait_ge(knrm_done, k + 1)
                nc.vector.tensor_reduce(k_n2[:], k_sq[:], AX_X, ALU.add).then_inc(kn2_done, 1)
                dve.wait_ge(knrm_done, k + 2)
                nc.vector.reciprocal(k_inv[:], k_nrm[:]).then_inc(kinv_done, 1)
                dve.wait_ge(kinv_done, k + 2)
                nc.vector.tensor_tensor(kn1[:, p, :, 0:M], k_sb[:],
                                        k_inv[:].unsqueeze(2).broadcast_to([128, SUB, M]),
                                        ALU.mult).then_inc(kn_done, 1)

            def add_outer(b, r):
                k = b * NCH + r
                dve.wait_ge(mat_mm, k + 3)
                dve.wait_ge(mat_done, k + 1)
                nc.vector.tensor_tensor(mat[:], mat[:], mat_ps[0:KU, 0:C + 1], ALU.add).then_inc(mat_done, 1)

            dve.sem_inc(kn_done, 1)
            dve.sem_inc(knrm_done, 1)
            dve.sem_inc(mat_mm, 2)
            with dve.Fori(0, B) as b:
                dve.wait_ge(mat_stored, 16 * b + 16)
                nc.vector.memset(mat[:], 0.0).then_inc(mat_zero, 1)
                dve.wait_ge(mat_zero, b + 1)
                keys(b, 0, 0)
                with dve.Fori(0, NCH // 2 - 1) as j:
                    for i in range(2):
                        keys(b, 2 * j + 1 + i, (1 + i) % 2)
                        add_outer(b, 2 * j + i)
                keys(b, NCH - 1, 1)
                add_outer(b, NCH - 2)
                add_outer(b, NCH - 1)


def phase_b(nc, t, uq, mat_dram, gmat_dram, un_dram, o_dram, stats):
    with ExitStack() as ctx:
        def sb(name, shape, dt=F32):
            return ctx.enter_context(nc.sbuf_tensor(name, shape, dt))

        def ps(name, shape):
            return ctx.enter_context(nc.psum_tensor(name, shape, F32))

        def sem(name):
            return ctx.enter_context(nc.semaphore(name))

        w_in = sb("w_in", [C, 2 * DI])
        taps = sb("taps", [K2, DI])
        conv_b = sb("conv_b", [128, 2])
        w_x = sb("w_x", [128, 2, 128])
        w_dt = sb("w_dt", [32, DI])
        b_dt = sb("b_dt", [128, 2])
        a_log = sb("a_log", [128, 2, S])
        a_pos = sb("a_pos", [128, 2, S])
        a_neg = sb("a_neg", [128, 2, S])
        d_skip = sb("d_skip", [128, 2])
        w_out = sb("w_out", [128, 2, C])
        gamma = sb("gamma", [K2, 1])
        eps_col = sb("eps_col", [K2, 1])
        ones = sb("ones", [K2, KU])
        ident = sb("ident", [128, 128])
        spread = sb("spread", [128, 2 * S, 128], BF16)
        mat2 = sb("mat2", [K2, C + 1])
        gmat = sb("gmat", [128, C])
        gmat_t = sb("gmat_t", [C, K2])
        den_v = sb("den_v", [K2, 1])
        den_w = sb("den_w", [K2, 128])
        w_xh = sb("w_xh", [K2, DI])
        w_z = sb("w_z", [K2, DI])
        carry = sb("carry", [128, S, 2])
        u_t = sb("u_t", [K2, 2, CH])
        den = sb("den", [K2, CH])
        rden = sb("rden", [K2, CH])
        un = sb("un", [K2, CH])
        xc = sb("xc", [128, 2, 2, CH])
        zs = sb("zs", [128, 2, 2, CH])
        dt_low = sb("dt_low", [32, CH])
        bc_hi = sb("bc_hi", [128, CH], BF16)
        bc_r = sb("bc_r", [128, CH])
        bc_mid = sb("bc_mid", [128, CH], BF16)
        bc3 = sb("bc3", [128, 2, CH], BF16)
        v = sb("v", [128, 2, CH])
        v_pos = sb("v_pos", [128, 2, CH])
        v_abs = sb("v_abs", [128, 2, CH])
        ex = sb("ex", [128, 2, CH])
        lg = sb("lg", [128, 2, CH])
        ex1 = sb("ex1", [128, 2, CH])
        dt = sb("dt", [128, 2, 2, CH])
        dtx = sb("dtx", [128, 2, 2, CH])
        d_a = sb("d_a", [128, 2, 2, CH])
        c_sb = sb("c_sb", [128, 2, CH])
        dbx = sb("dbx", [128, 2, 2, CH])
        h = sb("h", [128, S, 2, CH])
        hc = sb("hc", [128, HC, 2, CH])
        y = sb("y", [128, 2, CH])
        o_sb = sb("o_sb", [128, CH])

        b_ps = ps("b_ps", [128, 2, CH])
        c_ps = ps("c_ps", [128, CH])
        y_ps = ps("y_ps", [128, 2, CH])
        p_ps = ps("p_ps", [128, 3, CH])

        AHEAD = dict(scan=4, hc_done=S, y_mm=2 * HC, c_copied=2, dbx_done=2)
        sems = {}

        def stage(name):
            sems[name] = sem("B_" + name)
            AHEAD.setdefault(name, 1)
            return sems[name]

        weights, consts, ready, mat_in = stage("weights"), stage("consts"), stage("ready"), stage("mat_in")
        built = stage("built")
        gmat_done, den_v_done, den_w_done = stage("gmat_done"), stage("den_v_done"), stage("den_w_done")
        turn_mm, turned, fold_mm = stage("turn_mm"), stage("turned"), stage("fold_mm")
        fold_xh, fold_z, gmat_stored = stage("fold_xh"), stage("fold_z"), stage("gmat_stored")
        u_in0, u_in1 = stage("u_in0"), stage("u_in1")
        den_mm, den_max, den_rec = stage("den_mm"), stage("den_max"), stage("den_rec")
        un_done, un_stored = stage("un_done"), stage("un_stored")
        xh_mm = [stage("xh_mm0"), stage("xh_mm1")]
        z_mm = [stage("z_mm0"), stage("z_mm1")]
        xh_silu = [stage("xh_silu0"), stage("xh_silu1")]
        z_silu = [stage("z_silu0"), stage("z_silu1")]
        wx_mm, low_done, hi3_done, hi_done = stage("wx_mm"), stage("low_done"), stage("hi3_done"), stage("hi_done")
        rest_done, mid3_done, mid_done, lo3_done = (stage("rest_done"), stage("mid3_done"), stage("mid_done"),
                                                    stage("lo3_done"))
        dt_mm = [stage("dt_mm0"), stage("dt_mm1")]
        v_done = [stage("v_done0"), stage("v_done1")]
        pos_done, abs_done = stage("pos_done"), stage("abs_done")
        exp_done, log_done, plus_done, max_done = (stage("exp_done"), stage("log_done"), stage("plus_done"),
                                                  stage("max_done"))
        rec_done, ratio_done, log1p_done = stage("rec_done"), stage("ratio_done"), stage("log1p_done")
        dt_done, dtx_done = stage("dt_done"), stage("dtx_done")
        b_mm, c_mm, a_done, c_copied = stage("b_mm"), stage("c_mm"), stage("a_done"), stage("c_copied")
        dbx_done, scan, hc_done, y_mm = stage("dbx_done"), stage("scan"), stage("hc_done"), stage("y_mm")
        carried, skip_done, gate_done = stage("carried"), stage("skip_done"), stage("gate_done")
        out_mm, o_copied, bn_done, o_stored = stage("out_mm"), stage("o_copied"), stage("bn_done"), stage("o_stored")
        u_in = [u_in0, u_in1]

        def after(eng, name, runs):
            eng.wait_ge(sems[name], runs + AHEAD[name])

        block = ctx.enter_context(nc.Block())

        @block.sync
        def _(sp):
            for name, n in AHEAD.items():
                if n and name in sems:
                    sp.sem_inc(sems[name], n)
            after(sp, "consts", 8)
            for dst, src in ((w_in[:], t["w_in"]), (conv_b[:], t["conv_b"]), (b_dt[:], t["b_dt"]),
                             (a_log[:], t["a_log"]), (d_skip[:], t["d_skip"]), (w_out[:], t["w_out"]),
                             (w_dt[0:R], t["w_dt"]), (w_x[:, :, 0:R], t["w_x"][:, :, 0:R]),
                             (w_x[:, :, 32:64], t["w_x"][:, :, R:]), (w_x[:, :, 64:96], t["w_x"][:, :, R:]),
                             (w_x[:, :, 96:128], t["w_x"][:, :, R:]),
                             (taps[0:32], t["conv_w"][1].partition_broadcast(32)),
                             (taps[32:K2], t["conv_w"][0].partition_broadcast(KU)),
                             (gamma[:], t["gamma"].partition_broadcast(K2))):
                sp.dma_start(dst, src).then_inc(weights, 16)

            def load_u(b, c, p):
                after(sp, "un_done", b * SLOTS + c - 1)
                c0 = (b * SLOTS + 1 + c) * CH
                sp.dma_start(u_t[0:KU, p], uq[:, bass.ds(c0, CH)]).then_inc(u_in[p], 16)
                sp.dma_start(u_t[32:K2, p], uq[:, bass.ds(c0 - 1, CH)]).then_inc(u_in[p], 16)

            def store_un(b, c):
                after(sp, "un_done", b * SLOTS + c + 1)
                sp.dma_start(un_dram[:, bass.ds((b * SLOTS + c) * CH, CH)], un[0:KU]).then_inc(un_stored, 16)

            def store_o(km):
                after(sp, "o_copied", km + 1)
                sp.dma_start(o_dram[:, bass.ds(km * CH, CH)], o_sb[:]).then_inc(o_stored, 16)

            with sp.Fori(0, B) as b:
                after(sp, "gmat_done", b)
                after(sp, "den_v_done", b)
                for rows in (slice(0, KU), slice(32, K2)):
                    sp.dma_start(mat2[rows], mat_dram[bass.ds(b, 1)].rearrange("o k c -> (o k) c")
                                 ).then_inc(mat_in, 16)
                load_u(b, 0, 0)
                after(sp, "gmat_done", b + 1)
                sp.dma_start(gmat_dram[bass.ds(b, 1)].rearrange("o k c -> (o k) c"), gmat[0:KU]
                             ).then_inc(gmat_stored, 16)
                store_un(b, 0)
                with sp.Fori(0, NCH // 2) as j:
                    for p in range(2):
                        load_u(b, 2 * j + p + 1, 1 - p)
                        store_un(b, 2 * j + p + 1)
                        store_o(b * NCH + 2 * j + p)
            store_o(B * NCH)
            after(sp, "o_stored", 16 * (B * NCH + 1))
            after(sp, "un_stored", 16 * B * SLOTS)
            after(sp, "gmat_stored", 16 * B)

        @block.gpsimd
        def _(pool):
            pool.memset(ident[:], 0.0).then_inc(built, 1)
            pool.memset(spread[:], 0.0).then_inc(built, 1)
            after(pool, "built", 2)
            pool.affine_select(out=ident[:], in_=ident[:], compare_op=ALU.not_equal, fill=1.0, base=0,
                               pattern=[[-1, 128]], channel_multiplier=1).then_inc(built, 1)
            for i in range(3):
                after(pool, "built", 3 + i)
                pool.affine_select(out=spread[:], in_=spread[:], compare_op=ALU.not_equal, fill=1.0,
                                   base=-32 * (i + 1), pattern=[[-1, 2 * S], [0, 128]], channel_multiplier=1
                                   ).then_inc(built, 1)

            with pool.Fori(0, B * NCH) as km:
                for n in range(S):
                    i = km * S + n
                    after(pool, "scan", 2 * i + 2)
                    after(pool, "c_copied", i + 1)
                    after(pool, "y_mm", 2 * (i + 1 - HC))
                    nc.gpsimd.tensor_tensor(hc[:, n % HC], h[:, n],
                                            c_sb[:, n % 2].unsqueeze(1).broadcast_to([128, 2, CH]),
                                            ALU.mult).then_inc(hc_done, 1)

        @block.scalar
        def _(act):
            after(act, "ready", 1)
            nc.scalar.activation(a_pos[:], a_log[:], ACT.Exp).then_inc(ready, 1)
            after(act, "ready", 3)

            def silus(kp, p, gated):
                after(act, "gate_done", 2 * gated)
                for half in range(2):
                    after(act, f"xh_mm{half}", kp + 1)
                    nc.scalar.activation(xc[:, p, half], p_ps[:, 1 + half], ACT.Silu, bias=conv_b[:, half:half + 1]
                                         ).then_inc(xh_silu[half], 1)
                for half in range(2):
                    after(act, f"z_mm{half}", kp + 1)
                    nc.scalar.activation(zs[:, p, half], p_ps[:, half], ACT.Silu).then_inc(z_silu[half], 1)

            def high_parts(kp, p, bcasts):
                after(act, "wx_mm", kp + 1)
                after(act, "dt_mm1", kp)
                nc.scalar.activation(dt_low[:], p_ps[0:32, 2], ACT.Copy).then_inc(low_done, 1)
                after(act, "rest_done", kp)
                nc.scalar.activation(bc_hi[64:128], p_ps[64:128, 2], ACT.Copy).then_inc(hi_done, 1)
                after(act, "c_mm", bcasts)
                nc.scalar.activation(bc3[32:64, p], p_ps[32:64, 2], ACT.Copy).then_inc(hi3_done, 1)

            def middle_parts(kp, p):
                after(act, "rest_done", kp + 1)
                after(act, "lo3_done", kp)
                nc.scalar.activation(bc_mid[96:128], bc_r[96:128], ACT.Copy).then_inc(mid_done, 1)
                nc.scalar.activation(bc3[64:96, p], bc_r[64:96], ACT.Copy).then_inc(mid3_done, 1)

            def biased(kp):
                after(act, "pos_done", kp)
                after(act, "abs_done", kp)
                for half in range(2):
                    after(act, f"dt_mm{half}", kp + 1)
                    nc.scalar.activation(v[:, half], p_ps[:, half], ACT.Identity, bias=b_dt[:, half:half + 1]
                                         ).then_inc(v_done[half], 1)

            def softplus(kp):
                after(act, "abs_done", kp + 1)
                after(act, "log1p_done", kp)
                nc.scalar.activation(ex[:], v_abs[:], ACT.Exp, scale=-1.0).then_inc(exp_done, 1)
                after(act, "plus_done", kp + 1)
                after(act, "dt_done", kp)
                nc.scalar.activation(lg[:], ex1[:], ACT.Ln).then_inc(log_done, 1)

            def state(b, km, n, p):
                i = km * S + n
                if n == 0:
                    after(act, "dt_done", b + km + 1)
                for half in range(2):
                    after(act, "scan", 2 * (i - 2) + half + 1)
                    nc.scalar.activation(d_a[:, n % 2, half], dt[:, p, half], ACT.Exp,
                                         scale=a_neg[:, half, n:n + 1]).then_inc(a_done, 1)
                after(act, "c_mm", b + i + 1)
                after(act, "hc_done", i - 1)
                nc.scalar.activation(c_sb[:, n % 2], c_ps[:], ACT.Copy).then_inc(c_copied, 1)

            def copy_out(km):
                after(act, "out_mm", km + 1)
                after(act, "o_stored", 16 * km)
                after(act, "bn_done", km)
                nc.scalar.activation(o_sb[:], p_ps[:, 2], ACT.Copy).then_inc(o_copied, 1)

            with act.Fori(0, B) as b:
                silus(b * SLOTS, 0, b * NCH)
                high_parts(b * SLOTS, 0, b * (NCH * S + 1))
                middle_parts(b * SLOTS, 0)
                biased(b * SLOTS)
                softplus(b * SLOTS)
                with act.Fori(0, NCH // 2) as j:
                    for p in range(2):
                        km = b * NCH + 2 * j + p
                        kp = km + b + 1
                        for n in range(S):
                            state(b, km, n, p)
                            if n == 3:
                                silus(kp, 1 - p, km + 1)
                            if n == 5:
                                copy_out(km)
                            if n == 7:
                                high_parts(kp, 1 - p, b + km * S)
                            if n == 9:
                                middle_parts(kp, 1 - p)
                                biased(kp)
                            if n == 11:
                                softplus(kp)
            copy_out(B * NCH)

        @block.tensor
        def _(pe):
            after(pe, "weights", 16 * 14)
            after(pe, "built", 6)

            def fold(b):
                after(pe, "gmat_done", b + 1)
                after(pe, "rest_done", b * SLOTS)
                after(pe, "hi3_done", b * SLOTS)
                after(pe, "o_copied", b * NCH)
                nc.tensor.transpose(p_ps[:, 2, 0:128], gmat[:], ident[:]).then_inc(turn_mm, 1)
                after(pe, "turned", b + 1)
                nc.tensor.matmul(p_ps[0:K2, 2], gmat_t[:], w_in[:], start=True, stop=True).then_inc(fold_mm, 1)

            def denominator(b, kp, p, loads):
                after(pe, "den_w_done", 2 * b + 2)
                after(pe, f"u_in{p}", 32 * loads)
                after(pe, "v_done0", kp)
                nc.tensor.matmul(p_ps[:, 0], den_w[:], u_t[:, p], start=True, stop=True).then_inc(den_mm, 1)

            def inner(b, kp, half):
                after(pe, "fold_xh", b + 1)
                after(pe, "fold_z", b + 1)
                after(pe, "un_done", kp + 1)
                if half == 0:
                    after(pe, "v_done1", kp)
                else:
                    after(pe, "rest_done", kp)
                    after(pe, "hi3_done", kp)
                nc.tensor.matmul(p_ps[:, 1 + half], w_xh[:, 128 * half:128 * half + 128], un[:], start=True, stop=True
                                 ).then_inc(xh_mm[half], 1)

            def gate(kp, half):
                if half == 0:
                    after(pe, "den_max", kp + 1)
                else:
                    after(pe, "xh_silu0", kp + 1)
                nc.tensor.matmul(p_ps[:, half], w_z[:, 128 * half:128 * half + 128], un[:], start=True, stop=True
                                 ).then_inc(z_mm[half], 1)

            def project_x(kp, p, outs):
                after(pe, "xh_silu0", kp + 1)
                after(pe, "xh_silu1", kp + 1)
                after(pe, "o_copied", outs)
                for half in range(2):
                    last = nc.tensor.matmul(p_ps[:, 2], w_x[:, half], xc[:, p, half], start=(half == 0),
                                            stop=(half == 1))
                last.then_inc(wx_mm, 1)

            def project_dt(kp):
                after(pe, "low_done", kp + 1)
                for half in range(2):
                    after(pe, f"z_silu{half}", kp + 1)
                    nc.tensor.matmul(p_ps[:, half], w_dt[:, 128 * half:128 * half + 128], dt_low[:],
                                     start=True, stop=True).then_inc(dt_mm[half], 1)

            def spread_b(b, i, n, p):
                after(pe, "dbx_done", i - 1)
                after(pe, "b_mm", 2 * b + i)
                nc.tensor.matmul(b_ps[:, n % 2], spread[:, n], bc3[:, p], start=True, stop=True).then_inc(b_mm, 1)

            def spread_c(b, i, n, p):
                after(pe, "c_copied", i)
                nc.tensor.matmul(c_ps[:], spread[:, S + n], bc3[:, p], start=True, stop=True).then_inc(c_mm, 1)

            def split_done(kp):
                after(pe, "hi3_done", kp + 1)
                after(pe, "mid3_done", kp + 1)
                after(pe, "lo3_done", kp + 1)

            def add_state(km, n):
                i = km * S + n
                after(pe, "hc_done", i + 1)
                if n == 0:
                    after(pe, "skip_done", 2 * km + 2)
                for half in range(2):
                    nc.tensor.matmul(y_ps[:, half], ident[:], hc[:, n % HC, half], start=(n == 0), stop=(n == S - 1)
                                     ).then_inc(y_mm, 1)

            def out_product(km, kp):
                after(pe, "gate_done", 2 * km + 2)
                after(pe, "xh_silu1", kp + 1)
                for half in range(2):
                    last = nc.tensor.matmul(p_ps[:, 2], w_out[:, half], y[:, half], start=(half == 0),
                                            stop=(half == 1))
                last.then_inc(out_mm, 1)

            with pe.Fori(0, B) as b:
                kp = b * SLOTS
                fold(b)
                denominator(b, kp, 0, b * (NCH // 2 + 1) + 1)
                inner(b, kp, 0)
                inner(b, kp, 1)
                gate(kp, 0)
                gate(kp, 1)
                project_x(kp, 0, b * NCH)
                project_dt(kp)
                split_done(kp)
                spread_b(b, b * NCH * S, 0, 0)
                spread_b(b, b * NCH * S + 1, 1, 0)
                spread_c(b, b * NCH * S, 0, 0)
                with pe.Fori(0, NCH // 2) as j:
                    for p in range(2):
                        km = b * NCH + 2 * j + p
                        kp = km + b + 1
                        for n in range(S):
                            if n == S - 2:
                                split_done(kp)
                            i = km * S + n
                            if n == 0:
                                denominator(b, kp, 1 - p, b * (NCH // 2) + j + 1 if p == 0
                                            else b * (NCH // 2 + 1) + j + 2)
                            if n == 2:
                                inner(b, kp, 0)
                                inner(b, kp, 1)
                                gate(kp, 0)
                            if n == 3:
                                gate(kp, 1)
                            spread_b(b, i + 2, (n + 2) % S, p if n + 2 < S else 1 - p)
                            spread_c(b, i + 1, (n + 1) % S, p if n + 1 < S else 1 - p)
                            if n == 4:
                                out_product(km, kp)
                            if n == 6:
                                project_x(kp, 1 - p, km + 1)
                            if n == 8:
                                project_dt(kp)
                            if n >= 2:
                                add_state(km, n - 2)
                        add_state(km, S - 2)
                        add_state(km, S - 1)
            out_product(B * NCH, B * SLOTS - 1)

        @block.vector
        def _(dve):
            nc.vector.memset(w_x[:], 0.0).then_inc(consts, 1)
            nc.vector.memset(w_dt[:], 0.0).then_inc(consts, 1)
            nc.vector.memset(mat2[:], 0.0).then_inc(consts, 1)
            nc.vector.memset(u_t[:], 0.0).then_inc(consts, 1)
            nc.vector.memset(w_z[:], 0.0).then_inc(consts, 1)
            nc.vector.memset(bc3[:], 0.0).then_inc(consts, 1)
            nc.vector.memset(den_w[:], 0.0).then_inc(consts, 1)
            nc.vector.memset(ones[:], 1.0).then_inc(consts, 1)
            nc.vector.memset(xc[:], 0.0).then_inc(consts, 1)
            nc.vector.memset(zs[:], 0.0).then_inc(consts, 1)
            nc.vector.memset(y_ps[:], 0.0).then_inc(consts, 1)
            nc.vector.memset(eps_col[:], 0.0).then_inc(consts, 1)
            nc.vector.memset(gmat[:], 0.0).then_inc(consts, 1)
            after(dve, "consts", 13)
            for r0 in (0, 32):
                nc.vector.memset(eps_col[r0:r0 + M], LAYER0_EPS).then_inc(consts, 1)
            after(dve, "consts", 15)
            after(dve, "weights", 16 * 14)
            nc.vector.tensor_scalar(a_log[:], a_log[:], A_LOG_MAX, None, ALU.min).then_inc(ready, 1)
            after(dve, "ready", 2)
            nc.vector.tensor_scalar(a_neg[:], a_pos[:], -1.0, None, ALU.mult).then_inc(ready, 1)

            def fold(b):
                after(dve, "mat_in", 32 * (b + 1))
                after(dve, "turn_mm", b)
                after(dve, "gmat_stored", 16 * b)
                nc.vector.tensor_scalar(gmat[0:K2], mat2[:, 0:C], gamma[:], None, ALU.mult).then_inc(gmat_done, 1)
                after(dve, "den_w_done", 2 * b)
                nc.vector.tensor_tensor(den_v[:], mat2[:, C:C + 1], eps_col[:], ALU.add).then_inc(den_v_done, 1)
                after(dve, "den_v_done", b + 1)
                after(dve, "den_mm", b * SLOTS)
                for r0 in (0, 32):
                    nc.vector.tensor_scalar(den_w[r0:r0 + KU, r0:r0 + KU], ones[r0:r0 + KU], den_v[r0:r0 + KU, 0:1],
                                            None, ALU.mult).then_inc(den_w_done, 1)
                after(dve, "turn_mm", b + 1)
                after(dve, "fold_mm", b)
                nc.vector.tensor_copy(gmat_t[:], p_ps[:, 2, 0:K2]).then_inc(turned, 1)
                after(dve, "fold_mm", b + 1)
                after(dve, "xh_mm1", b * SLOTS)
                after(dve, "z_mm1", b * SLOTS)
                nc.vector.tensor_tensor(w_xh[:], p_ps[0:K2, 2, 0:DI], taps[:], ALU.mult).then_inc(fold_xh, 1)
                nc.vector.tensor_copy(w_z[0:32], p_ps[0:32, 2, DI:2 * DI]).then_inc(fold_z, 1)

            def den_bound(kp):
                after(dve, "den_mm", kp + 1)
                after(dve, "den_rec", kp)
                nc.vector.tensor_scalar(den[:], p_ps[0:K2, 0], TINY, None, ALU.max).then_inc(den_max, 1)

            def den_reciprocal(kp):
                after(dve, "den_max", kp + 1)
                after(dve, "un_done", kp)
                nc.vector.reciprocal(rden[:], den[:]).then_inc(den_rec, 1)

            def divide(kp, p):
                after(dve, "den_rec", kp + 1)
                after(dve, "xh_mm1", kp)
                after(dve, "z_mm1", kp)
                after(dve, "un_stored", 16 * kp)
                nc.vector.tensor_tensor(un[:], u_t[:, p], rden[:], ALU.mult).then_inc(un_done, 1)

            def rest(kp):
                after(dve, "hi_done", kp + 1)
                after(dve, "mid_done", kp)
                after(dve, "mid3_done", kp)
                after(dve, "lo3_done", kp)
                nc.vector.tensor_tensor(bc_r[64:128], p_ps[64:128, 2], bc_hi[64:128], ALU.subtract
                                        ).then_inc(rest_done, 1)

            def low_part(kp, p):
                after(dve, "mid_done", kp + 1)
                nc.vector.tensor_tensor(bc3[96:128, p], bc_r[96:128], bc_mid[96:128], ALU.subtract
                                        ).then_inc(lo3_done, 1)

            def absolute(kp):
                after(dve, "v_done0", kp + 1)
                after(dve, "v_done1", kp + 1)
                after(dve, "exp_done", kp)
                nc.vector.scalar_tensor_tensor(out=v_abs[:], in0=v[:], scalar=-1.0, in1=v[:], op0=ALU.mult, op1=ALU.max
                                               ).then_inc(abs_done, 1)

            def positive(kp):
                after(dve, "dt_done", kp)
                nc.vector.tensor_scalar(v_pos[:], v[:], 0.0, None, ALU.max).then_inc(pos_done, 1)

            def plus_one(kp):
                after(dve, "exp_done", kp + 1)
                after(dve, "ratio_done", kp)
                nc.vector.tensor_scalar(ex1[:], ex[:], 1.0, None, ALU.add).then_inc(plus_done, 1)

            def bound(kp):
                after(dve, "log_done", kp + 1)
                nc.vector.tensor_scalar(ex1[:], ex1[:], -1.0, LOG_MIN, ALU.add, ALU.max).then_inc(max_done, 1)

            def invert(kp):
                after(dve, "max_done", kp + 1)
                nc.vector.reciprocal(ex1[:], ex1[:]).then_inc(rec_done, 1)

            def ratio(kp):
                after(dve, "rec_done", kp + 1)
                nc.vector.scalar_tensor_tensor(out=lg[:], in0=lg[:], scalar=LOG_MIN, in1=ex1[:], op0=ALU.max, op1=ALU.mult
                                               ).then_inc(ratio_done, 1)

            def log1p(kp):
                after(dve, "ratio_done", kp + 1)
                nc.vector.tensor_tensor(lg[:], lg[:], ex[:], ALU.mult).then_inc(log1p_done, 1)

            def make_dt(kp, p):
                after(dve, "log1p_done", kp + 1)
                after(dve, "pos_done", kp + 1)
                nc.vector.tensor_tensor(dt[:, p], lg[:], v_pos[:], ALU.add).then_inc(dt_done, 1)

            def make_dtx(kp, p):
                after(dve, "dt_done", kp + 1)
                after(dve, "xh_silu1", kp + 1)
                nc.vector.tensor_tensor(dtx[:, p], dt[:, p], xc[:, p], ALU.mult).then_inc(dtx_done, 1)

            def skip(km, half, p):
                after(dve, "y_mm", 2 * S * km)
                after(dve, "out_mm", km)
                nc.vector.scalar_tensor_tensor(out=y[:, half], in0=xc[:, p, half], scalar=d_skip[:, half:half + 1],
                                               in1=y_ps[:, half], op0=ALU.mult, op1=ALU.add).then_inc(skip_done, 1)

            def gate(km, half, p):
                after(dve, "skip_done", 2 * km + 1 + half)
                nc.vector.tensor_tensor(y[:, half], y[:, half], zs[:, p, half], ALU.mult).then_inc(gate_done, 1)

            def statistics(km):
                after(dve, "o_copied", km + 1)
                nc.vector.bn_stats(stats[:, bass.ds(km, 1), :].rearrange("c o s -> c (o s)"), o_sb[:]
                                   ).then_inc(bn_done, 1)

            def weigh(b, km, n, p):
                i = km * S + n
                if n == 0:
                    after(dve, "dtx_done", b + km + 1)
                after(dve, "b_mm", 2 * b + i + 1)
                after(dve, "scan", 2 * (i - 1))
                nc.vector.tensor_tensor(dbx[:, n % 2], dtx[:, p], b_ps[:, n % 2].unsqueeze(1).broadcast_to([128, 2, CH]),
                                        ALU.mult).then_inc(dbx_done, 1)

            def run_scan(km, n, half):
                i = km * S + n
                after(dve, "dbx_done", i + 1)
                after(dve, "a_done", 2 * i + half + 1)
                after(dve, "hc_done", i - S + 1)
                nc.vector.tensor_tensor_scan(h[:, n, half], d_a[:, n % 2, half], dbx[:, n % 2, half],
                                             carry[:, n, half:half + 1], ALU.mult, ALU.add).then_inc(scan, 1)

            def prelude(kp, p):
                den_bound(kp)
                den_reciprocal(kp)
                divide(kp, p)
                rest(kp)
                low_part(kp, p)
                absolute(kp)
                positive(kp)
                plus_one(kp)
                bound(kp)
                invert(kp)
                ratio(kp)
                log1p(kp)
                make_dt(kp, p)
                make_dtx(kp, p)

            with dve.Fori(0, B) as b:
                fold(b)
                after(dve, "carried", b + b * NCH)
                nc.vector.memset(carry[:], 0.0).then_inc(carried, 1)
                prelude(b * SLOTS, 0)
                with dve.Fori(0, NCH // 2) as j:
                    for p in range(2):
                        km = b * NCH + 2 * j + p
                        kp = km + b + 1
                        o = 1 - p
                        steps = {
                            0: (lambda: den_bound(kp), lambda: den_reciprocal(kp)),
                            1: (lambda: divide(kp, o), lambda: skip(km, 0, o)),
                            2: (lambda: skip(km, 1, o), lambda: gate(km, 0, o)),
                            3: (lambda: gate(km, 1, o), None),
                            6: (lambda: statistics(km), None),
                            8: (lambda: rest(kp), None),
                            10: (lambda: low_part(kp, o), lambda: absolute(kp)),
                            11: (lambda: positive(kp), lambda: plus_one(kp)),
                            12: (lambda: bound(kp), lambda: invert(kp)),
                            13: (lambda: ratio(kp), lambda: log1p(kp)),
                            14: (lambda: make_dt(kp, o), lambda: make_dtx(kp, o)),
                        }
                        weigh(b, km, 0, p)
                        after(dve, "carried", b + km + 1)
                        for n in range(S):
                            first, second = steps.get(n, (None, None))
                            if n + 1 < S:
                                weigh(b, km, n + 1, p)
                            if first:
                                first()
                            run_scan(km, n, 0)
                            if second:
                                second()
                            run_scan(km, n, 1)
                        after(dve, "scan", 2 * S * (km + 1))
                        nc.vector.tensor_copy(carry[:], h[:, :, :, CH - 1]).then_inc(carried, 1)
            skip(B * NCH, 0, 1)
            skip(B * NCH, 1, 1)
            gate(B * NCH, 0, 1)
            gate(B * NCH, 1, 1)
            statistics(B * NCH)


def phase_c(nc, t, gmat_dram, un_dram, o_dram, stats, out):
    with ExitStack() as ctx:
        def sb(name, shape, dt=F32):
            return ctx.enter_context(nc.sbuf_tensor(name, shape, dt))

        def sem(name):
            return ctx.enter_context(nc.semaphore(name))

        gn = sb("gn", [C, 2])
        share = sb("share", [C, C])
        eps = sb("gn_eps", [C, 1])
        moments = sb("moments", [C, B, 2])
        m2 = sb("m2", [C, B])
        g_mv = sb("g_mv", [C, B, 2])
        g_m2 = sb("g_m2", [C, B])
        g_std = sb("g_std", [C, B])
        scale = sb("scale", [C, B])
        shift = sb("shift", [C, B])
        ab = sb("ab", [C, 2, 2])
        gm = sb("gm_c", [KU, B, C])
        gm_b = sb("gm_b", [KU, 2, C])
        o_t = sb("o_t", [C, 2, CB])
        u_t = sb("u_c", [KU, 2, CB])
        act_t = sb("act_t", [C, 2, CB])
        r_t = sb("r_t", [C, 2, CB])
        res_ps = ctx.enter_context(nc.psum_tensor("res_ps", [C, 2, CB], F32))

        small_in = sem("C_small_in")
        step = sem("C_step")
        share_mm = sem("C_share_mm")
        rooted = sem("C_rooted")
        o_in = [sem(f"C_o_in{p}") for p in range(2)]
        u_in = [sem(f"C_u_in{p}") for p in range(2)]
        ab_done = sem("C_ab_done")
        gm_done = sem("C_gm_done")
        silu_done = sem("C_silu_done")
        res_mm = sem("C_res_mm")
        added = sem("C_added")
        stored = [sem(f"C_stored{p}") for p in range(2)]
        block = ctx.enter_context(nc.Block())

        @block.sync
        def _(sp):
            sp.dma_start(gn[:], t["gn"]).then_inc(small_in, 16)
            sp.dma_start(gm[:], gmat_dram.rearrange("b k c -> k b c")).then_inc(small_in, 16)
            sp.sem_inc(silu_done, 2)
            sp.sem_inc(res_mm, 2)
            for p in range(2):
                sp.sem_inc(stored[p], 16)
            with sp.Fori(0, B) as b:
                with sp.Fori(0, NCB // 2) as j:
                    for p in range(2):
                        k = b * NCB + 2 * j + p
                        c0 = (2 * j + p) * CB
                        sp.wait_ge(silu_done, k + 1)
                        sp.dma_start(o_t[:, p], o_dram[:, bass.ds((b * NCH + 1) * CH + c0, CB)]).then_inc(o_in[p], 16)
                        sp.wait_ge(res_mm, k + 1)
                        sp.dma_start(u_t[:, p], un_dram[:, bass.ds(b * SLOTS * CH + c0, CB)]).then_inc(u_in[p], 16)

        @block.scalar
        def _(act):
            act.wait_ge(step, STEPS_BEFORE_ROOT)
            nc.scalar.activation(g_std[:], g_m2[:], ACT.Sqrt, bias=eps[:]).then_inc(rooted, 1)
            with act.Fori(0, B) as b:
                act.wait_ge(ab_done, 2 * b + 2)
                with act.Fori(0, NCB // 2) as j:
                    for p in range(2):
                        k = b * NCB + 2 * j + p
                        act.wait_ge(o_in[p], 16 * (b * (NCB // 2) + j + 1))
                        act.wait_ge(added, k + 1)
                        nc.scalar.activation(act_t[:, p], o_t[:, p], ACT.Silu, bias=ab[:, 1, 0:1], scale=ab[:, 0, 0:1]
                                             ).then_inc(silu_done, 1)
                        act.wait_ge(added, k + 3)
                        act.dma_start(out[bass.ds(b, 1), :, bass.ds((2 * j + p) * CB, CB)]
                                      .rearrange("o c n -> (o c) n"), r_t[:, p]).then_inc(stored[p], 16)
            for p in range(2):
                act.wait_ge(stored[p], 16 * (B * NCB // 2 + 1))

        @block.tensor
        def _(pe):
            pe.wait_ge(step, STEPS_BEFORE_SHARE)
            nc.tensor.matmul(res_ps[:, 0, 0:2 * B], share[:], moments[:].rearrange("c b s -> c (b s)"),
                             start=True, stop=True).then_inc(share_mm, 1)
            pe.wait_ge(step, STEPS_BEFORE_ROOT)
            with pe.Fori(0, B) as b:
                with pe.Fori(0, NCB // 2) as j:
                    for p in range(2):
                        pe.wait_ge(gm_done, b + 1)
                        k = b * NCB + 2 * j + p
                        pe.wait_ge(u_in[p], 16 * (b * (NCB // 2) + j + 1))
                        pe.wait_ge(added, k + 1)
                        for i in range(CB // CH):
                            last = nc.tensor.matmul(res_ps[:, p, CH * i:CH * i + CH], gm_b[:, 0],
                                                    u_t[:, p, CH * i:CH * i + CH], start=True, stop=True)
                        last.then_inc(res_mm, 1)

        @block.vector
        def _(dve):
            done = [0]

            def chain(ins):
                done[0] += 1
                ins.then_inc(step, 1)
                dve.wait_ge(step, done[0])

            chain(nc.vector.memset(share[:], 0.0))
            for g in range(C // GROUP):
                s = slice(GROUP * g, GROUP * g + GROUP)
                chain(nc.vector.memset(share[s, s], 1.0 / GROUP))
            chain(nc.vector.memset(eps[:], GN_EPS))
            for b in range(B):
                chain(nc.vector.bn_aggr(moments[:, b], stats[:, b * NCH + 1:(b + 1) * NCH + 1, :]
                                        .rearrange("c k s -> c (k s)")))
            chain(nc.vector.tensor_tensor(m2[:], moments[:, :, 0], moments[:, :, 0], ALU.mult))
            chain(nc.vector.tensor_tensor(moments[:, :, 1], moments[:, :, 1], m2[:], ALU.add))
            assert done[0] == STEPS_BEFORE_SHARE
            dve.wait_ge(share_mm, 1)
            chain(nc.vector.tensor_copy(g_mv[:].rearrange("c b s -> c (b s)"), res_ps[:, 0, 0:2 * B]))
            chain(nc.vector.tensor_tensor(m2[:], g_mv[:, :, 0], g_mv[:, :, 0], ALU.mult))
            chain(nc.vector.tensor_tensor(g_m2[:], g_mv[:, :, 1], m2[:], ALU.subtract))
            assert done[0] == STEPS_BEFORE_ROOT
            dve.wait_ge(rooted, 1)
            dve.wait_ge(small_in, 32)
            chain(nc.vector.reciprocal(m2[:], g_std[:]))
            chain(nc.vector.tensor_scalar(scale[:], m2[:], gn[:, 0:1], None, ALU.mult))
            chain(nc.vector.tensor_tensor(m2[:], g_mv[:, :, 0], scale[:], ALU.mult))
            chain(nc.vector.tensor_scalar(shift[:], m2[:], -1.0, gn[:, 1:2], ALU.mult, ALU.add))
            dve.sem_inc(added, 2)
            with dve.Fori(0, B) as b:
                dve.wait_ge(silu_done, b * NCB + 2)
                dve.wait_ge(res_mm, b * NCB + 2)
                nc.vector.tensor_copy(ab[:, 0, 0:1], scale[:, bass.ds(b, 1)]).then_inc(ab_done, 1)
                nc.vector.tensor_copy(ab[:, 1, 0:1], shift[:, bass.ds(b, 1)]).then_inc(ab_done, 1)
                nc.vector.tensor_copy(gm_b[:, 0], gm[:, bass.ds(b, 1), :].rearrange("k o c -> k (o c)")
                                      ).then_inc(gm_done, 1)
                with dve.Fori(0, NCB // 2) as j:
                    for p in range(2):
                        k = b * NCB + 2 * j + p
                        dve.wait_ge(silu_done, k + 3)
                        dve.wait_ge(res_mm, k + 3)
                        dve.wait_ge(stored[p], 16 * (b * (NCB // 2) + j + 1))
                        nc.vector.tensor_tensor(r_t[:, p], act_t[:, p], res_ps[:, p], ALU.add).then_inc(added, 1)


STEPS_BEFORE_SHARE = 1 + C // GROUP + 1 + B + 2
STEPS_BEFORE_ROOT = STEPS_BEFORE_SHARE + 3


def build(nc, t, out):
    uq = nc.dram_tensor("uq", (KU, (B * SLOTS + 1) * CH), F32, kind="Internal").ap()
    un_dram = nc.dram_tensor("un_dram", (KU, B * SLOTS * CH), F32, kind="Internal").ap()
    o_dram = nc.dram_tensor("o_dram", (C, (B * NCH + 1) * CH), F32, kind="Internal").ap()
    mat_dram = nc.dram_tensor("mat_dram", (B, KU, C + 1), F32, kind="Internal").ap()
    gmat_dram = nc.dram_tensor("gmat_dram", (B, KU, C), F32, kind="Internal").ap()
    phase_a(nc, t, uq, mat_dram)
    with nc.sbuf_tensor("stats", [C, B * NCH + 1, 6], F32) as stats:
        phase_b(nc, t, uq, mat_dram, gmat_dram, un_dram, o_dram, stats)
        phase_c(nc, t, gmat_dram, un_dram, o_dram, stats, out)


def kernel(x, **w):
    import numpy as np
    import concourse.bacc as bacc
    from concourse.bass_utils import run_bass_kernel_spmd

    l0 = {k[8:]: np.asarray(v) for k, v in w.items() if k.startswith("L0_conv_")}
    l1 = {k[8:]: np.asarray(v) for k, v in w.items() if k.startswith("L1_conv_")}
    dil = [l0["w2"], l0["w3"], l0["w4"]]
    at = [(dy + 1, dx + 1) for dy, dx in TAPS]
    arrays = {
        "x": np.asarray(x),
        "w_center": np.concatenate([l0["w1"][:, :, 0, 0]] + [v[:, :, 1, 1] for v in dil]).T,
        "w_taps": np.stack([np.stack([v[:, :, i, j].T for i, j in at], 1) for v in dil], 1),
        "w_kv": np.concatenate([l0["wk"][:, :, 0, 0], l0["wv"][:, :, 0, 0]]).T,
        "b_kv": np.concatenate([l0["bk"], l0["bv"]]),
        "w_q": l0["wq"][:, :, 0, 0].T,
        "b_q": l0["bq"][:, None],
        "bn": np.stack([l0["bn_scale"].ravel(), l0["bn_bias"].ravel(), l0["bn_mean"].ravel(),
                        l0["bn_var"].ravel()], 1),
        "gamma": l0["gamma"],
        "w_in": l1["W_in"],
        "conv_w": l1["conv_w"].T,
        "conv_b": l1["conv_b"].reshape(2, 128).T,
        "w_x": l1["W_x"].reshape(2, 128, R + 2 * S).transpose(1, 0, 2),
        "w_dt": l1["W_dt"],
        "b_dt": l1["b_dt"].reshape(2, 128).T,
        "a_log": l1["A_log"].reshape(2, 128, S).transpose(1, 0, 2),
        "d_skip": l1["D"].reshape(2, 128).T,
        "w_out": l1["W_out"].reshape(2, 128, C).transpose(1, 0, 2),
        "gn": np.stack([l1["gn_gamma"], l1["gn_beta"]], 1),
    }
    arrays = {k: np.ascontiguousarray(v) for k, v in arrays.items()}
    nc = bacc.Bacc("TRN2", target_bir_lowering=False, num_devices=1)
    t = {k: nc.dram_tensor("in_" + k, v.shape, F32, kind="ExternalInput").ap() for k, v in arrays.items()}
    out = nc.dram_tensor("out", (B, C, N), F32, kind="ExternalOutput").ap()
    build(nc, t, out)
    r = run_bass_kernel_spmd(nc, [{"in_" + k: v for k, v in arrays.items()}], core_ids=[0])
    return r.results[0]["out"].reshape(B, C, H, W)
```

```python
from contextlib import ExitStack

import concourse.bass as bass
from concourse import mybir

F32 = mybir.dt.float32
BF16 = mybir.dt.bfloat16
ALU = mybir.AluOpType
ACT = mybir.ActivationFunctionType
AX_X = mybir.AxisListType.X

B, C, H, W = 8, 128, 128, 128
N = H * W
M = 16
CH = 512
ROWS = CH // W
NCH = N // CH
SUB = CH // 128
PAD = 18
WP = W + 2 * PAD
BR = 32
DIL = (6, 12, 18)
TAPS = [(dy, dx) for dy in (-1, 0, 1) for dx in (-1, 0, 1) if (dy, dx) != (0, 0)]
KU = M + 1
K2 = 32 + KU
DI = 256
S = 16
R = 8
SLOTS = NCH + 1
LAYER0_EPS, BN_EPS, GN_EPS = 1e-6, 1e-5, 1e-5
GROUP = 32
TINY = 1e-18
A_LOG_MAX = 81.5
PIECE = 8
PIECES = H // PIECE
HC = 4
CB = 2048
NCB = N // CB


def phase_a(nc, t, uq, mat_dram):
    with ExitStack() as ctx:
        def sb(name, shape, dt=F32):
            return ctx.enter_context(nc.sbuf_tensor(name, shape, dt))

        def ps(name, shape):
            return ctx.enter_context(nc.psum_tensor(name, shape, F32))

        def sem(name):
            return ctx.enter_context(nc.semaphore(name))

        image = sb("image", [C, WP, WP])
        w_center = sb("w_center", [C, 4 * BR])
        w_taps = sb("w_taps", [C, 3, 8, BR])
        w_kv = sb("w_kv", [C, M + C])
        w_q = sb("w_q", [C, M])
        b_kv = sb("b_kv", [128, M + C])
        b_q = sb("b_q", [M, 1])
        bn = sb("bn", [C, 4])
        bn_std = sb("bn_std", [C, 1])
        bn_inv = sb("bn_inv", [C, 1])
        bn_mi = sb("bn_mi", [C, 1])
        bn_shift = sb("bn_shift", [C, 1])
        bn_eps = sb("bn_eps", [C, 1])
        ones_m = sb("ones_m", [M, 64])
        zero_chunk = sb("zero_chunk", [KU, CH])
        x_q = sb("x_q", [C, CH])
        q_sb = sb("q_sb", [M, 2, CH])
        s_sb = sb("s_sb", [65, 2, CH])
        q_sq = sb("q_sq", [M, CH])
        k_sb = sb("k_sb", [128, SUB, M])
        k_sq = sb("k_sq", [128, SUB, M])
        k_n2 = sb("k_n2", [128, SUB])
        k_nrm = sb("k_nrm", [128, SUB])
        k_inv = sb("k_inv", [128, SUB])
        kn1 = sb("kn1", [128, 2, SUB, KU])
        v1 = sb("v1", [128, 2, SUB, C + 1])
        mat = sb("mat", [KU, C + 1])

        conv_ps = ps("conv_ps", [128, 2, CH])
        kv_ps = ps("kv_ps", [128, 2, 2, CH])
        qs_ps = ps("qs_ps", [128, CH])
        mat_ps = ps("mat_ps", [128, CH])

        weights = sem("weights")
        cleared = sem("cleared")
        set_up = sem("set_up")
        bn_root = sem("bn_root")
        pads_stored = sem("pads_stored")
        x_loaded = sem("x_loaded")
        conv_done = sem("conv_done")
        bn_done = sem("bn_done")
        kv_done = sem("kv_done")
        k_done = sem("k_done")
        ksq_done = sem("ksq_done")
        kn2_done = sem("kn2_done")
        v_done = sem("v_done")
        knrm_done = sem("knrm_done")
        kinv_done = sem("kinv_done")
        kn_done = sem("kn_done")
        q_mm = sem("q_mm")
        q_done = sem("q_done")
        sq_done = sem("sq_done")
        s2_mm = sem("s2_mm")
        s_done = sem("s_done")
        u_stored = [sem(f"u_stored{p}") for p in range(2)]
        mat_mm = sem("mat_mm")
        mat_done = sem("mat_done")
        mat_zero = sem("mat_zero")
        mat_stored = sem("mat_stored")

        block = ctx.enter_context(nc.Block())

        @block.sync
        def _(sp):
            for dst, src in ((w_center[:], t["w_center"]), (w_taps[:], t["w_taps"]), (w_kv[:], t["w_kv"]),
                             (w_q[:], t["w_q"]), (b_kv[:], t["b_kv"].partition_broadcast(128)),
                             (b_q[:], t["b_q"]), (bn[:], t["bn"])):
                sp.dma_start(dst, src).then_inc(weights, 16)
            sp.wait_ge(cleared, 5)
            for i in range(4):
                rows = slice(i * 32, i * 32 + 32)
                sp.dma_start(image[:, PAD + 32 * i:PAD + 32 * i + 32, PAD:PAD + W],
                             t["x"][0, :, rows, :]).then_inc(x_loaded, 16)
            for b in range(B + 1):
                sp.dma_start(uq[:, b * SLOTS * CH:b * SLOTS * CH + CH], zero_chunk[:]).then_inc(pads_stored, 16)

            with sp.Fori(1, B) as b:
                with sp.Fori(0, PIECES - 3) as j:
                    sp.wait_ge(conv_done, (b - 1) * NCH + 2 * j + 7)
                    sp.dma_start(image[:, bass.ds(j * PIECE + PAD, PIECE), PAD:PAD + W],
                                 t["x"][bass.ds(b, 1), :, bass.ds(j * PIECE, PIECE), :]
                                 .rearrange("o c h w -> (o c) h w")).then_inc(x_loaded, 16)
                sp.wait_ge(conv_done, b * NCH)
                rest = (PIECES - 3) * PIECE
                sp.dma_start(image[:, PAD + rest:PAD + H, PAD:PAD + W],
                             t["x"][bass.ds(b, 1), :, rest:H, :]
                             .rearrange("o c h w -> (o c) h w")).then_inc(x_loaded, 16)
            sp.wait_ge(pads_stored, 16 * (B + 1))
            sp.wait_ge(x_loaded, 16 * (4 + (B - 1) * (PIECES - 2)))

        def loaded(eng, b):
            eng.wait_ge(x_loaded, 16 * 4 + b * (16 * (PIECES - 2)))

        @block.gpsimd
        def _(pool):
            pool.memset(image[:], 0.0).then_inc(cleared, 1)
            pool.memset(zero_chunk[:], 0.0).then_inc(cleared, 1)
            pool.memset(ones_m[:], 1.0).then_inc(cleared, 1)
            pool.memset(kn1[:], 1.0).then_inc(cleared, 1)
            pool.memset(v1[:], 1.0).then_inc(cleared, 1)
            for p in range(2):
                pool.sem_inc(u_stored[p], 32)
            pool.sem_inc(mat_stored, 16)

        @block.scalar
        def _(act):
            act.wait_ge(weights, 16 * 7)
            act.wait_ge(set_up, 1)
            nc.scalar.activation(bn_std[:], bn[:, 3:4], ACT.Sqrt, bias=bn_eps[:]).then_inc(bn_root, 1)
            act.sem_inc(bn_done, 2)
            act.sem_inc(s_done, 1)
            act.wait_ge(set_up, 5)

            def relu(b, r, p):
                act.wait_ge(conv_done, b * NCH + r + 1)
                act.wait_ge(q_mm, b * NCH + r + 1)
                nc.scalar.activation(x_q[:], conv_ps[:, p], ACT.Relu, bias=bn_shift[:], scale=bn_inv[:]
                                     ).then_inc(bn_done, 1)

            def norms(b, r, p):
                k = b * NCH + r
                act.wait_ge(kn2_done, k + 1)
                act.wait_ge(kinv_done, k + 1)
                nc.scalar.activation(k_nrm[:], k_n2[:], ACT.Sqrt).then_inc(knrm_done, 1)

            def query(b, j, p):
                r = 2 * j + p
                k = b * NCH + r
                act.wait_ge(q_mm, k + 2)
                act.wait_ge(u_stored[p], 32 * (b * (NCH // 2) + j + 1))
                nc.scalar.activation(q_sb[:, p], qs_ps[0:M, :], ACT.Identity, bias=b_q[:]).then_inc(q_done, 1)
                act.wait_ge(s2_mm, k + 1)
                nc.scalar.activation(q_sq[:], qs_ps[0:M, :], ACT.Square, bias=b_q[:]).then_inc(sq_done, 1)
                act.wait_ge(s2_mm, k + 2)
                nc.scalar.activation(s_sb[64:65, p], qs_ps[64:65, :], ACT.Sqrt).then_inc(s_done, 1)
                act.wait_ge(q_done, k + 1)
                act.wait_ge(s_done, k + 2)
                c0 = (b * SLOTS + r + 1) * CH
                act.dma_start(uq[0:M, bass.ds(c0, CH)], q_sb[:, p]).then_inc(u_stored[p], 16)
                act.dma_start(uq[M:KU, bass.ds(c0, CH)], s_sb[64:65, p]).then_inc(u_stored[p], 16)

            with act.Fori(0, B) as b:
                with act.Fori(0, NCH // 2) as j:
                    for p in range(2):
                        relu(b, 2 * j + p, p)
                        norms(b, 2 * j + p, p)
                        query(b, j, p)
                act.wait_ge(mat_done, (b + 1) * NCH + 1)
                act.dma_start(mat_dram[bass.ds(b, 1), :, :].rearrange("o k c -> (o k) c"), mat[:]
                              ).then_inc(mat_stored, 16)
            for p in range(2):
                act.wait_ge(u_stored[p], 32 * (B * NCH // 2 + 1))
            act.wait_ge(mat_stored, 16 * (B + 1))

        @block.tensor
        def _(pe):
            pe.wait_ge(weights, 16 * 7)
            pe.wait_ge(cleared, 5)
            pe.sem_inc(q_mm, 1)
            pe.sem_inc(s2_mm, 1)

            def kv(b, r, p):
                k = b * NCH + r
                pe.wait_ge(v_done, k + 1)
                for j in range(SUB):
                    last = nc.tensor.matmul(kv_ps[:, p, j // 2, (j % 2) * (M + C):(j % 2 + 1) * (M + C)],
                                            image[:, PAD + ROWS * r + j, PAD:PAD + W], w_kv[:], start=True, stop=True)
                last.then_inc(kv_done, 1)

            def conv(b, r, p):
                k = b * NCH + r
                pe.wait_ge(bn_done, k + 1)
                y0 = r * ROWS + PAD
                nc.tensor.matmul(conv_ps[:, p], w_center[:], image[:, y0:y0 + ROWS, PAD:PAD + W],
                                 start=True, stop=False, skip_group_check=True)
                steps = [(n, i) for n, (dy, _) in enumerate(TAPS) for i, d in enumerate(DIL)
                         if -ROWS < r * ROWS + dy * d < H]
                for n, i in steps:
                    y1, x1 = y0 + TAPS[n][0] * DIL[i], PAD + TAPS[n][1] * DIL[i]
                    last = nc.tensor.matmul(conv_ps[BR * (i + 1):BR * (i + 2), p], w_taps[:, i, n, :],
                                            image[:, y1:y1 + ROWS, x1:x1 + W],
                                            start=False, stop=(n == 7), skip_group_check=True)
                last.then_inc(conv_done, 1)

            def query(b, r, p):
                k = b * NCH + r
                pe.wait_ge(bn_done, k + 3)
                pe.wait_ge(s_done, k + 1)
                nc.tensor.matmul(qs_ps[0:M, :], w_q[:], x_q[:], start=True, stop=True).then_inc(q_mm, 1)

            def query_norm(b, r, p):
                k = b * NCH + r
                pe.wait_ge(sq_done, k + 1)
                nc.tensor.matmul(qs_ps[64:128, :], ones_m[:], q_sq[:], start=True, stop=True).then_inc(s2_mm, 1)

            def outer(b, r, p):
                k = b * NCH + r
                pe.wait_ge(kn_done, k + 2)
                pe.wait_ge(mat_done, k + 1)
                for j in range(SUB):
                    last = nc.tensor.matmul(mat_ps[0:KU, 0:C + 1], kn1[:, p, j, :], v1[:, p, j, :],
                                            start=(j == 0), stop=(j == SUB - 1))
                last.then_inc(mat_mm, 1)

            with pe.Fori(0, B) as b:
                loaded(pe, b)
                for r in range(NCH + 1):
                    p = r % 2
                    if r < NCH:
                        kv(b, r, p)
                    if r > 0:
                        query(b, r - 1, 1 - p)
                    if r < NCH:
                        conv(b, r, p)
                    if r > 0:
                        query_norm(b, r - 1, 1 - p)
                        outer(b, r - 1, 1 - p)

        @block.vector
        def _(dve):
            nc.vector.memset(bn_eps[:], BN_EPS).then_inc(set_up, 1)
            dve.wait_ge(bn_root, 1)
            nc.vector.reciprocal(bn_mi[:], bn_std[:]).then_inc(set_up, 1)
            dve.wait_ge(set_up, 2)
            nc.vector.tensor_tensor(bn_inv[:], bn_mi[:], bn[:, 0:1], ALU.mult).then_inc(set_up, 1)
            dve.wait_ge(set_up, 3)
            nc.vector.tensor_tensor(bn_mi[:], bn[:, 2:3], bn_inv[:], ALU.mult).then_inc(set_up, 1)
            dve.wait_ge(set_up, 4)
            nc.vector.tensor_tensor(bn_shift[:], bn[:, 1:2], bn_mi[:], ALU.subtract).then_inc(set_up, 1)
            dve.wait_ge(cleared, 5)
            dve.sem_inc(v_done, 2)
            dve.sem_inc(kinv_done, 1)
            dve.sem_inc(mat_done, 1)

            def keys(b, r, p):
                k = b * NCH + r
                dve.wait_ge(kv_done, k + 1)
                kv = kv_ps[:, p, :, 0:2 * (M + C)].rearrange("t a (j e) -> t a j e", j=2)
                dve.wait_ge(kn_done, k + 1)
                nc.vector.tensor_tensor(k_sb[:].rearrange("t (a j) m -> t a j m", a=2), kv[:, :, :, 0:M],
                                        b_kv[:, 0:M].unsqueeze(1).unsqueeze(1).broadcast_to([128, 2, 2, M]),
                                        ALU.add).then_inc(k_done, 1)
                dve.wait_ge(mat_mm, k + 1)
                nc.vector.tensor_tensor(v1[:, p, :, 0:C].rearrange("t (a j) c -> t a j c", a=2), kv[:, :, :, M:M + C],
                                        b_kv[:, M:M + C].unsqueeze(1).unsqueeze(1).broadcast_to([128, 2, 2, C]),
                                        ALU.add).then_inc(v_done, 1)
                dve.wait_ge(k_done, k + 1)
                nc.vector.tensor_tensor(k_sq[:], k_sb[:], k_sb[:], ALU.mult).then_inc(ksq_done, 1)
                dve.wait_ge(ksq_done, k + 1)
                dve.wait_ge(knrm_done, k + 1)
                nc.vector.tensor_reduce(k_n2[:], k_sq[:], AX_X, ALU.add).then_inc(kn2_done, 1)
                dve.wait_ge(knrm_done, k + 2)
                nc.vector.reciprocal(k_inv[:], k_nrm[:]).then_inc(kinv_done, 1)
                dve.wait_ge(kinv_done, k + 2)
                nc.vector.tensor_tensor(kn1[:, p, :, 0:M], k_sb[:],
                                        k_inv[:].unsqueeze(2).broadcast_to([128, SUB, M]),
                                        ALU.mult).then_inc(kn_done, 1)

            def add_outer(b, r):
                k = b * NCH + r
                dve.wait_ge(mat_mm, k + 3)
                dve.wait_ge(mat_done, k + 1)
                nc.vector.tensor_tensor(mat[:], mat[:], mat_ps[0:KU, 0:C + 1], ALU.add).then_inc(mat_done, 1)

            dve.sem_inc(kn_done, 1)
            dve.sem_inc(knrm_done, 1)
            dve.sem_inc(mat_mm, 2)
            with dve.Fori(0, B) as b:
                dve.wait_ge(mat_stored, 16 * b + 16)
                nc.vector.memset(mat[:], 0.0).then_inc(mat_zero, 1)
                dve.wait_ge(mat_zero, b + 1)
                keys(b, 0, 0)
                with dve.Fori(0, NCH // 2 - 1) as j:
                    for i in range(2):
                        keys(b, 2 * j + 1 + i, (1 + i) % 2)
                        add_outer(b, 2 * j + i)
                keys(b, NCH - 1, 1)
                add_outer(b, NCH - 2)
                add_outer(b, NCH - 1)


def phase_b(nc, t, uq, mat_dram, gmat_dram, un_dram, o_dram, stats):
    with ExitStack() as ctx:
        def sb(name, shape, dt=F32):
            return ctx.enter_context(nc.sbuf_tensor(name, shape, dt))

        def ps(name, shape):
            return ctx.enter_context(nc.psum_tensor(name, shape, F32))

        def sem(name):
            return ctx.enter_context(nc.semaphore(name))

        DA = 4
        w_in = sb("w_in", [C, 2 * DI])
        taps = sb("taps", [K2, DI])
        conv_b = sb("conv_b", [128, 2])
        w_x = sb("w_x", [128, 2, 128])
        w_dt = sb("w_dt", [32, DI])
        b_dt = sb("b_dt", [128, 2])
        a_log = sb("a_log", [128, 2, S])
        a_pos = sb("a_pos", [128, 2, S])
        a_neg = sb("a_neg", [128, 2, S])
        d_skip = sb("d_skip", [128, 2])
        w_out = sb("w_out", [128, 2, C])
        gamma = sb("gamma", [K2, 1])
        eps_col = sb("eps_col", [K2, 1])
        one_col = sb("one_col", [128, 1])
        ones = sb("ones", [K2, KU])
        ident = sb("ident", [128, 128])
        spread = sb("spread", [128, 2 * S, 128], BF16)
        mat2 = sb("mat2", [K2, C + 1])
        gmat = sb("gmat", [128, C])
        gmat_t = sb("gmat_t", [C, K2])
        den_v = sb("den_v", [K2, 1])
        den_w = sb("den_w", [K2, 128])
        w_xh = sb("w_xh", [K2, DI])
        w_z = sb("w_z", [K2, DI])
        carry = sb("carry", [128, S, 2])
        u_t = sb("u_t", [K2, 2, CH])
        rden0 = sb("rden0", [K2, CH])
        den_r = sb("den_r", [K2, CH])
        un = sb("un", [K2, CH])
        xc = sb("xc", [128, 2, 2, CH])
        zs = sb("zs", [128, 2, 2, CH])
        bc_hi = sb("bc_hi", [128, CH], BF16)
        bc_r = sb("bc_r", [128, CH])
        dt_low = bc_r[0:32]
        bc_mid = sb("bc_mid", [128, CH], BF16)
        bc3 = sb("bc3", [128, 2, CH], BF16)
        v = sb("v", [128, 2, CH])
        ex = sb("ex", [128, 2, CH])
        lg = sb("lg", [128, 2, CH])
        ex1 = sb("ex1", [128, 2, CH])
        den = ex1[0:K2, 0]
        ex_r = sb("ex_r", [128, 2, CH])
        dt = sb("dt", [128, 2, 2, CH])
        dtx = sb("dtx", [128, 2, 2, CH])
        d_a = sb("d_a", [128, DA, 2, CH])
        c_sb = sb("c_sb", [128, 2, CH])
        dbx = sb("dbx", [128, 2, 2, CH])
        h = sb("h", [128, S, 2, CH])
        hc = sb("hc", [128, HC, 2, CH])
        y = sb("y", [128, 2, CH])
        o_sb = sb("o_sb", [128, CH])

        b_ps = ps("b_ps", [128, 2, CH])
        c_ps = ps("c_ps", [128, CH])
        y_ps = ps("y_ps", [128, 2, CH])
        p_ps = ps("p_ps", [128, 3, CH])

        LAG = 2
        AHEAD = dict(scan=2 * DA, a_done=2 * DA, hc_done=S, y_mm=2 * HC, c_copied=2, dbx_done=2)
        sems = {}

        def stage(name):
            sems[name] = sem("B_" + name)
            AHEAD.setdefault(name, 1)
            return sems[name]

        weights, consts, ready, mat_in = stage("weights"), stage("consts"), stage("ready"), stage("mat_in")
        built = stage("built")
        gmat_done, den_v_done, den_w_done = stage("gmat_done"), stage("den_v_done"), stage("den_w_done")
        turn_mm, turned, fold_mm = stage("turn_mm"), stage("turned"), stage("fold_mm")
        fold_xh, fold_z, gmat_stored = stage("fold_xh"), stage("fold_z"), stage("gmat_stored")
        u_in0, u_in1 = stage("u_in0"), stage("u_in1")
        den_mm, den_max, den_rec = stage("den_mm"), stage("den_max"), stage("den_rec")
        den_log, den_exp, den_res = stage("den_log"), stage("den_exp"), stage("den_res")
        un_done, un_stored = stage("un_done"), stage("un_stored")
        xh_mm = [stage("xh_mm0"), stage("xh_mm1")]
        z_mm = [stage("z_mm0"), stage("z_mm1")]
        xh_silu = [stage("xh_silu0"), stage("xh_silu1")]
        z_silu = [stage("z_silu0"), stage("z_silu1")]
        wx_mm, low_done, hi3_done, hi_done = stage("wx_mm"), stage("low_done"), stage("hi3_done"), stage("hi_done")
        rest_done, mid3_done, mid_done, lo3_done = (stage("rest_done"), stage("mid3_done"), stage("mid_done"),
                                                    stage("lo3_done"))
        dt_mm = [stage("dt_mm0"), stage("dt_mm1")]
        v_done = [stage("v_done0"), stage("v_done1")]
        abs_done, exp_done, plus_done = stage("abs_done"), stage("exp_done"), stage("plus_done")
        log_done, rest1_done, log1p_done = stage("log_done"), stage("rest1_done"), stage("log1p_done")
        dt_done, dtx_done = stage("dt_done"), stage("dtx_done")
        b_mm, c_mm, a_done, c_copied = stage("b_mm"), stage("c_mm"), stage("a_done"), stage("c_copied")
        dbx_done, scan, hc_done, y_mm = stage("dbx_done"), stage("scan"), stage("hc_done"), stage("y_mm")
        carried, skip_done, gate_done = stage("carried"), stage("skip_done"), stage("gate_done")
        out_mm, o_copied, bn_done, o_stored = stage("out_mm"), stage("o_copied"), stage("bn_done"), stage("o_stored")
        u_in = [u_in0, u_in1]

        def after(eng, name, runs):
            eng.wait_ge(sems[name], runs + AHEAD[name])

        block = ctx.enter_context(nc.Block())

        @block.sync
        def _(sp):
            for name, n in AHEAD.items():
                if name == "y_mm":
                    n -= 2 * LAG
                sp.sem_inc(sems[name], n)
            after(sp, "consts", 8)
            for dst, src in ((w_in[:], t["w_in"]), (conv_b[:], t["conv_b"]), (b_dt[:], t["b_dt"]),
                             (a_log[:], t["a_log"]), (d_skip[:], t["d_skip"]), (w_out[:], t["w_out"]),
                             (w_dt[0:R], t["w_dt"]), (w_x[:, :, 0:R], t["w_x"][:, :, 0:R]),
                             (w_x[:, :, 32:64], t["w_x"][:, :, R:]), (w_x[:, :, 64:96], t["w_x"][:, :, R:]),
                             (w_x[:, :, 96:128], t["w_x"][:, :, R:]),
                             (taps[0:32], t["conv_w"][1].partition_broadcast(32)),
                             (taps[32:K2], t["conv_w"][0].partition_broadcast(KU)),
                             (gamma[:], t["gamma"].partition_broadcast(K2))):
                sp.dma_start(dst, src).then_inc(weights, 16)

            def load_u(b, c, p):
                after(sp, "un_done", b * SLOTS + c - 1)
                c0 = (b * SLOTS + 1 + c) * CH
                sp.dma_start(u_t[0:KU, p], uq[:, bass.ds(c0, CH)]).then_inc(u_in[p], 16)
                sp.dma_start(u_t[32:K2, p], uq[:, bass.ds(c0 - 1, CH)]).then_inc(u_in[p], 16)

            def store_un(b, c):
                after(sp, "un_done", b * SLOTS + c + 1)
                sp.dma_start(un_dram[:, bass.ds((b * SLOTS + c) * CH, CH)], un[0:KU]).then_inc(un_stored, 16)

            def store_o(km):
                after(sp, "o_copied", km + 1)
                sp.dma_start(o_dram[:, bass.ds(km * CH, CH)], o_sb[:]).then_inc(o_stored, 16)

            with sp.Fori(0, B) as b:
                after(sp, "gmat_done", b)
                after(sp, "den_v_done", b)
                for rows in (slice(0, KU), slice(32, K2)):
                    sp.dma_start(mat2[rows], mat_dram[bass.ds(b, 1)].rearrange("o k c -> (o k) c")
                                 ).then_inc(mat_in, 16)
                load_u(b, 0, 0)
                after(sp, "gmat_done", b + 1)
                sp.dma_start(gmat_dram[bass.ds(b, 1)].rearrange("o k c -> (o k) c"), gmat[0:KU]
                             ).then_inc(gmat_stored, 16)
                store_un(b, 0)
                with sp.Fori(0, NCH // 2) as j:
                    for p in range(2):
                        load_u(b, 2 * j + p + 1, 1 - p)
                        store_un(b, 2 * j + p + 1)
                        store_o(b * NCH + 2 * j + p)
            store_o(B * NCH)
            after(sp, "o_stored", 16 * (B * NCH + 1))
            after(sp, "un_stored", 16 * B * SLOTS)
            after(sp, "gmat_stored", 16 * B)

        @block.gpsimd
        def _(pool):
            pool.memset(ident[:], 0.0).then_inc(built, 1)
            pool.memset(spread[:], 0.0).then_inc(built, 1)
            after(pool, "built", 2)
            pool.affine_select(out=ident[:], in_=ident[:], compare_op=ALU.not_equal, fill=1.0, base=0,
                               pattern=[[-1, 128]], channel_multiplier=1).then_inc(built, 1)
            for i in range(3):
                after(pool, "built", 3 + i)
                pool.affine_select(out=spread[:], in_=spread[:], compare_op=ALU.not_equal, fill=1.0,
                                   base=-32 * (i + 1), pattern=[[-1, 2 * S], [0, 128]], channel_multiplier=1
                                   ).then_inc(built, 1)

            def weigh_out(km, n):
                i = km * S + n
                after(pool, "scan", 2 * i + 2)
                after(pool, "c_copied", i + 1)
                after(pool, "y_mm", 2 * (i + 1 - HC))
                nc.gpsimd.tensor_tensor(hc[:, n % HC], h[:, n],
                                        c_sb[:, n % 2].unsqueeze(1).broadcast_to([128, 2, CH]),
                                        ALU.mult).then_inc(hc_done, 1)

            def den_residual(kp):
                after(pool, "den_exp", kp + 1)
                after(pool, "un_done", kp)
                nc.gpsimd.tensor_tensor(den_r[:], den, rden0[:], ALU.mult).then_inc(den_res, 1)

            def log1p(kp):
                after(pool, "rest1_done", kp + 1)
                after(pool, "log_done", kp + 1)
                nc.gpsimd.tensor_tensor(lg[:], lg[:], ex_r[:], ALU.subtract).then_inc(log1p_done, 1)

            def make_dtx(kp, p):
                after(pool, "dt_done", kp + 1)
                after(pool, "xh_silu1", kp + 1)
                nc.gpsimd.tensor_tensor(dtx[:, p], dt[:, p], xc[:, p], ALU.mult).then_inc(dtx_done, 1)

            def gate(km, p):
                after(pool, "skip_done", 2 * km + 2)
                nc.gpsimd.tensor_tensor(y[:], y[:], zs[:, p], ALU.mult).then_inc(gate_done, 1)

            with pool.Fori(0, B) as b:
                den_residual(b * SLOTS)
                log1p(b * SLOTS)
                make_dtx(b * SLOTS, 0)
                with pool.Fori(0, NCH // 2) as j:
                    for p in range(2):
                        km = b * NCH + 2 * j + p
                        kp = km + b + 1
                        for n in range(S):
                            if n == 2:
                                den_residual(kp)
                            if n == 4:
                                gate(km, 1 - p)
                            if n == 12:
                                log1p(kp)
                            if n == 14:
                                make_dtx(kp, 1 - p)
                            weigh_out(km, n)
            gate(B * NCH, 1)

        @block.scalar
        def _(act):
            nc.scalar.preload_act_table_set("natural_log_exp_and_others")
            after(act, "ready", 1)
            nc.scalar.activation(a_pos[:], a_log[:], ACT.Exp).then_inc(ready, 1)
            after(act, "ready", 3)

            def invert(kp):
                after(act, "den_max", kp + 1)
                after(act, "den_rec", kp)
                nc.scalar.activation(rden0[:], den, ACT.Ln).then_inc(den_log, 1)
                after(act, "den_log", kp + 1)
                nc.scalar.activation(rden0[:], rden0[:], ACT.Exp, scale=-1.0).then_inc(den_exp, 1)

            def silu_x(kp, p, gated):
                after(act, "gate_done", gated)
                for half in range(2):
                    after(act, f"xh_mm{half}", kp + 1)
                    nc.scalar.activation(xc[:, p, half], p_ps[:, 1 + half], ACT.Silu, bias=conv_b[:, half:half + 1]
                                         ).then_inc(xh_silu[half], 1)

            def silu_z(kp, p):
                for half in range(2):
                    after(act, f"z_mm{half}", kp + 1)
                    nc.scalar.activation(zs[:, p, half], p_ps[:, half], ACT.Silu).then_inc(z_silu[half], 1)
                nc.scalar.preload_act_table_set("natural_log_exp_and_others")

            def high_parts(kp, p, bcasts):
                after(act, "wx_mm", kp + 1)
                after(act, "dt_mm1", kp)
                nc.scalar.activation(dt_low, p_ps[0:32, 2], ACT.Copy).then_inc(low_done, 1)
                after(act, "rest_done", kp)
                nc.scalar.activation(bc_hi[64:128], p_ps[64:128, 2], ACT.Copy).then_inc(hi_done, 1)
                after(act, "c_mm", bcasts)
                nc.scalar.activation(bc3[32:64, p], p_ps[32:64, 2], ACT.Copy).then_inc(hi3_done, 1)

            def middle_parts(kp, p):
                after(act, "rest_done", kp + 1)
                after(act, "lo3_done", kp)
                nc.scalar.activation(bc_mid[96:128], bc_r[96:128], ACT.Copy).then_inc(mid_done, 1)
                nc.scalar.activation(bc3[64:96, p], bc_r[64:96], ACT.Copy).then_inc(mid3_done, 1)

            def biased(kp):
                after(act, "dt_done", kp)
                after(act, "abs_done", kp)
                for half in range(2):
                    after(act, f"dt_mm{half}", kp + 1)
                    nc.scalar.activation(v[:, half], p_ps[:, half], ACT.Identity, bias=b_dt[:, half:half + 1]
                                         ).then_inc(v_done[half], 1)

            def exponential(kp):
                after(act, "v_done0", kp + 1)
                after(act, "v_done1", kp + 1)
                after(act, "rest1_done", kp)
                nc.scalar.activation(ex[:], v[:], ACT.Abs).then_inc(abs_done, 1)
                after(act, "abs_done", kp + 1)
                nc.scalar.activation(ex[:], ex[:], ACT.Exp, scale=-1.0).then_inc(exp_done, 1)

            def plus_one(kp):
                after(act, "exp_done", kp + 1)
                after(act, "rest1_done", kp)
                after(act, "log_done", kp)
                after(act, "den_res", kp + 1)
                nc.scalar.activation(ex1[:], ex[:], ACT.Identity, bias=one_col[:]).then_inc(plus_done, 1)

            def logarithm(kp):
                after(act, "plus_done", kp + 1)
                after(act, "dt_done", kp)
                nc.scalar.activation(lg[:], ex1[:], ACT.Ln).then_inc(log_done, 1)

            def decay(b, km, n, p):
                i = km * S + n
                if n == 0:
                    after(act, "dt_done", b + km + 1)
                for half in range(2):
                    after(act, "scan", 2 * (i - DA) + half + 1)
                    after(act, "a_done", 2 * (2 * b + i - DA) + half + 1)
                    nc.scalar.activation(d_a[:, n % DA, half], dt[:, p, half], ACT.Exp,
                                         scale=a_neg[:, half, n:n + 1]).then_inc(a_done, 1)

            def copy_c(b, km, n):
                i = km * S + n
                after(act, "c_mm", b + i + 1)
                after(act, "hc_done", i - 1)
                nc.scalar.activation(c_sb[:, n % 2], c_ps[:], ACT.Copy).then_inc(c_copied, 1)

            def copy_out(km):
                after(act, "out_mm", km + 1)
                after(act, "o_stored", 16 * km)
                after(act, "bn_done", km)
                nc.scalar.activation(o_sb[:], p_ps[:, 2], ACT.Copy).then_inc(o_copied, 1)

            with act.Fori(0, B) as b:
                invert(b * SLOTS)
                silu_x(b * SLOTS, 0, b * NCH)
                silu_z(b * SLOTS, 0)
                high_parts(b * SLOTS, 0, b * (NCH * S + 1))
                middle_parts(b * SLOTS, 0)
                biased(b * SLOTS)
                exponential(b * SLOTS)
                plus_one(b * SLOTS)
                logarithm(b * SLOTS)
                decay(b, b * NCH, 0, 0)
                decay(b, b * NCH, 1, 0)
                with act.Fori(0, NCH // 2) as j:
                    for p in range(2):
                        km = b * NCH + 2 * j + p
                        kp = km + b + 1
                        for n in range(S):
                            if n == 6:
                                copy_c(b, km, n)
                                silu_z(kp, 1 - p)
                            for m in {0: (2, 3), S - 3: (), S - 2: (S,), S - 1: (S + 1,)}.get(n, (n + 3,)):
                                decay(b, km + m // S, m % S, p if m < S else 1 - p)
                            if n != 6:
                                copy_c(b, km, n)
                            if n == 0:
                                invert(kp)
                            if n == 5:
                                silu_x(kp, 1 - p, km + 1)
                            if n == 7:
                                high_parts(kp, 1 - p, b + km * S)
                            if n == 8:
                                biased(kp)
                                exponential(kp)
                            if n == 9:
                                plus_one(kp)
                                middle_parts(kp, 1 - p)
                            if n == 10:
                                logarithm(kp)
                            if n == 12:
                                copy_out(km)
            copy_out(B * NCH)

        @block.tensor
        def _(pe):
            after(pe, "weights", 16 * 14)
            after(pe, "built", 6)

            def fold(b):
                after(pe, "gmat_done", b + 1)
                after(pe, "rest_done", b * SLOTS)
                after(pe, "hi3_done", b * SLOTS)
                after(pe, "o_copied", b * NCH)
                nc.tensor.transpose(p_ps[:, 2, 0:128], gmat[:], ident[:]).then_inc(turn_mm, 1)
                after(pe, "turned", b + 1)
                nc.tensor.matmul(p_ps[0:K2, 2], gmat_t[:], w_in[:], start=True, stop=True).then_inc(fold_mm, 1)

            def denominator(b, kp, p, loads):
                after(pe, "den_w_done", 2 * b + 2)
                after(pe, f"u_in{p}", 32 * loads)
                after(pe, "v_done0", kp)
                nc.tensor.matmul(p_ps[:, 0], den_w[:], u_t[:, p], start=True, stop=True).then_inc(den_mm, 1)

            def inner(b, kp, half, outs):
                after(pe, "fold_xh", b + 1)
                after(pe, "fold_z", b + 1)
                after(pe, "un_done", kp + 1)
                if half == 0:
                    after(pe, "v_done1", kp)
                else:
                    after(pe, "rest_done", kp)
                    after(pe, "hi3_done", kp)
                    after(pe, "o_copied", outs)
                nc.tensor.matmul(p_ps[:, 1 + half], w_xh[:, 128 * half:128 * half + 128], un[:], start=True, stop=True
                                 ).then_inc(xh_mm[half], 1)

            def gate(kp, half):
                if half == 0:
                    after(pe, "den_max", kp + 1)
                else:
                    after(pe, "xh_silu0", kp + 1)
                nc.tensor.matmul(p_ps[:, half], w_z[:, 128 * half:128 * half + 128], un[:], start=True, stop=True
                                 ).then_inc(z_mm[half], 1)

            def project_x(kp, p):
                after(pe, "xh_silu0", kp + 1)
                after(pe, "xh_silu1", kp + 1)
                for half in range(2):
                    last = nc.tensor.matmul(p_ps[:, 2], w_x[:, half], xc[:, p, half], start=(half == 0),
                                            stop=(half == 1))
                last.then_inc(wx_mm, 1)

            def project_dt(kp):
                after(pe, "low_done", kp + 1)
                for half in range(2):
                    after(pe, f"z_silu{half}", kp + 1)
                    nc.tensor.matmul(p_ps[:, half], w_dt[:, 128 * half:128 * half + 128], dt_low,
                                     start=True, stop=True).then_inc(dt_mm[half], 1)

            def spread_b(b, i, n, p):
                after(pe, "dbx_done", i - 1)
                after(pe, "b_mm", 2 * b + i)
                nc.tensor.matmul(b_ps[:, n % 2], spread[:, n], bc3[:, p], start=True, stop=True).then_inc(b_mm, 1)

            def spread_c(b, i, n, p):
                after(pe, "c_copied", i)
                nc.tensor.matmul(c_ps[:], spread[:, S + n], bc3[:, p], start=True, stop=True).then_inc(c_mm, 1)

            def split_done(kp):
                after(pe, "hi3_done", kp + 1)
                after(pe, "mid3_done", kp + 1)
                after(pe, "lo3_done", kp + 1)

            def add_state(i, n):
                after(pe, "hc_done", i + 1)
                for half in range(2):
                    nc.tensor.matmul(y_ps[:, half], ident[:], hc[:, n % HC, half], start=(n == 0), stop=(n == S - 1)
                                     ).then_inc(y_mm, 1)

            def out_product(km, preludes):
                after(pe, "gate_done", km + 1)
                after(pe, "rest_done", preludes)
                after(pe, "hi3_done", preludes)
                for half in range(2):
                    last = nc.tensor.matmul(p_ps[:, 2], w_out[:, half], y[:, half], start=(half == 0),
                                            stop=(half == 1))
                last.then_inc(out_mm, 1)

            after(pe, "consts", 17)
            for half in range(2):
                nc.tensor.matmul(y_ps[:, half], ident[:], hc[:, HC - LAG, half], start=True, stop=False)

            with pe.Fori(0, B) as b:
                kp = b * SLOTS
                fold(b)
                denominator(b, kp, 0, b * (NCH // 2 + 1) + 1)
                inner(b, kp, 0, b * NCH)
                inner(b, kp, 1, b * NCH)
                gate(kp, 0)
                gate(kp, 1)
                project_x(kp, 0)
                project_dt(kp)
                split_done(kp)
                spread_b(b, b * NCH * S, 0, 0)
                spread_b(b, b * NCH * S + 1, 1, 0)
                spread_c(b, b * NCH * S, 0, 0)
                with pe.Fori(0, NCH // 2) as j:
                    for p in range(2):
                        km = b * NCH + 2 * j + p
                        kp = km + b + 1
                        for n in range(S):
                            if n == S - 2:
                                split_done(kp)
                            i = km * S + n
                            if n == 0:
                                denominator(b, kp, 1 - p, b * (NCH // 2) + j + 1 if p == 0
                                            else b * (NCH // 2 + 1) + j + 2)
                            spread_b(b, i + 2, (n + 2) % S, p if n + 2 < S else 1 - p)
                            if n == LAG + 1:
                                after(pe, "skip_done", 2 * km + 2)
                                add_state(i - LAG - 1, 0)
                            if n != LAG:
                                add_state(i - LAG, (n - LAG) % S)
                            spread_c(b, i + 1, (n + 1) % S, p if n + 1 < S else 1 - p)
                            if n == 4:
                                inner(b, kp, 0, km)
                                inner(b, kp, 1, km)
                            if n == 5:
                                gate(kp, 0)
                                gate(kp, 1)
                            if n == 6:
                                project_x(kp, 1 - p)
                            if n == 7:
                                project_dt(kp)
                            if n == 10:
                                out_product(km, kp + 1)
            for n in range(S - LAG, S):
                add_state((B * NCH - 1) * S + n, n)
            out_product(B * NCH, B * SLOTS)

        @block.vector
        def _(dve):
            nc.vector.memset(w_x[:], 0.0).then_inc(consts, 1)
            nc.vector.memset(w_dt[:], 0.0).then_inc(consts, 1)
            nc.vector.memset(mat2[:], 0.0).then_inc(consts, 1)
            nc.vector.memset(u_t[:], 0.0).then_inc(consts, 1)
            nc.vector.memset(w_z[:], 0.0).then_inc(consts, 1)
            nc.vector.memset(bc3[:], 0.0).then_inc(consts, 1)
            nc.vector.memset(den_w[:], 0.0).then_inc(consts, 1)
            nc.vector.memset(ones[:], 1.0).then_inc(consts, 1)
            nc.vector.memset(xc[:], 0.0).then_inc(consts, 1)
            nc.vector.memset(zs[:], 0.0).then_inc(consts, 1)
            nc.vector.memset(y[:], 0.0).then_inc(consts, 1)
            nc.vector.memset(hc[:, HC - LAG:HC], 0.0).then_inc(consts, 1)
            nc.vector.memset(eps_col[:], 0.0).then_inc(consts, 1)
            nc.vector.memset(one_col[:], 1.0).then_inc(consts, 1)
            nc.vector.memset(gmat[:], 0.0).then_inc(consts, 1)
            after(dve, "consts", 15)
            for r0 in (0, 32):
                nc.vector.memset(eps_col[r0:r0 + M], LAYER0_EPS).then_inc(consts, 1)
            after(dve, "consts", 17)
            after(dve, "weights", 16 * 14)
            nc.vector.tensor_scalar(a_log[:], a_log[:], A_LOG_MAX, None, ALU.min).then_inc(ready, 1)
            after(dve, "ready", 2)
            nc.vector.tensor_scalar(a_neg[:], a_pos[:], -1.0, None, ALU.mult).then_inc(ready, 1)

            def fold(b):
                after(dve, "mat_in", 32 * (b + 1))
                after(dve, "turn_mm", b)
                after(dve, "gmat_stored", 16 * b)
                nc.vector.tensor_scalar(gmat[0:K2], mat2[:, 0:C], gamma[:], None, ALU.mult).then_inc(gmat_done, 1)
                after(dve, "den_w_done", 2 * b)
                nc.vector.tensor_tensor(den_v[:], mat2[:, C:C + 1], eps_col[:], ALU.add).then_inc(den_v_done, 1)
                after(dve, "den_v_done", b + 1)
                after(dve, "den_mm", b * SLOTS)
                for r0 in (0, 32):
                    nc.vector.tensor_scalar(den_w[r0:r0 + KU, r0:r0 + KU], ones[r0:r0 + KU], den_v[r0:r0 + KU, 0:1],
                                            None, ALU.mult).then_inc(den_w_done, 1)
                after(dve, "turn_mm", b + 1)
                after(dve, "fold_mm", b)
                nc.vector.tensor_copy(gmat_t[:], p_ps[:, 2, 0:K2]).then_inc(turned, 1)
                after(dve, "fold_mm", b + 1)
                after(dve, "xh_mm1", b * SLOTS)
                after(dve, "z_mm1", b * SLOTS)
                nc.vector.tensor_tensor(w_xh[:], p_ps[0:K2, 2, 0:DI], taps[:], ALU.mult).then_inc(fold_xh, 1)
                nc.vector.tensor_copy(w_z[0:32], p_ps[0:32, 2, DI:2 * DI]).then_inc(fold_z, 1)

            def den_bound(kp):
                after(dve, "den_mm", kp + 1)
                after(dve, "den_res", kp)
                after(dve, "den_log", kp)
                after(dve, "log_done", kp)
                after(dve, "rest1_done", kp)
                nc.vector.tensor_scalar(den, p_ps[0:K2, 0], TINY, None, ALU.max).then_inc(den_max, 1)

            def den_reciprocal(kp):
                after(dve, "den_res", kp + 1)
                nc.vector.scalar_tensor_tensor(out=den_r[:], in0=den_r[:], scalar=-2.0, in1=rden0[:], op0=ALU.add,
                                               op1=ALU.mult).then_inc(den_rec, 1)

            def divide(kp, p):
                after(dve, "den_rec", kp + 1)
                after(dve, "xh_mm1", kp)
                after(dve, "z_mm1", kp)
                after(dve, "un_stored", 16 * kp)
                nc.vector.scalar_tensor_tensor(out=un[:], in0=den_r[:], scalar=-1.0, in1=u_t[:, p], op0=ALU.mult,
                                               op1=ALU.mult).then_inc(un_done, 1)

            def rest(kp):
                after(dve, "hi_done", kp + 1)
                after(dve, "mid_done", kp)
                after(dve, "mid3_done", kp)
                after(dve, "lo3_done", kp)
                nc.vector.tensor_tensor(bc_r[64:128], p_ps[64:128, 2], bc_hi[64:128], ALU.subtract
                                        ).then_inc(rest_done, 1)

            def low_part(kp, p):
                after(dve, "mid_done", kp + 1)
                nc.vector.tensor_tensor(bc3[96:128, p], bc_r[96:128], bc_mid[96:128], ALU.subtract
                                        ).then_inc(lo3_done, 1)

            def rounding(kp):
                after(dve, "plus_done", kp + 1)
                after(dve, "log1p_done", kp)
                nc.vector.scalar_tensor_tensor(out=ex_r[:], in0=ex1[:], scalar=-1.0, in1=ex[:], op0=ALU.add,
                                               op1=ALU.subtract).then_inc(rest1_done, 1)

            def make_dt(kp, p):
                after(dve, "log1p_done", kp + 1)
                nc.vector.scalar_tensor_tensor(out=dt[:, p], in0=v[:], scalar=0.0, in1=lg[:], op0=ALU.max,
                                               op1=ALU.add).then_inc(dt_done, 1)

            def skip(km, half, p):
                after(dve, "y_mm", 2 * S * km)
                after(dve, "out_mm", km)
                nc.vector.scalar_tensor_tensor(out=y[:, half], in0=xc[:, p, half], scalar=d_skip[:, half:half + 1],
                                               in1=y_ps[:, half], op0=ALU.mult, op1=ALU.add).then_inc(skip_done, 1)

            def statistics(km):
                after(dve, "o_copied", km + 1)
                nc.vector.bn_stats(stats[:, bass.ds(km, 1), :].rearrange("c o s -> c (o s)"), o_sb[:]
                                   ).then_inc(bn_done, 1)

            def weigh(b, km, n, p):
                i = km * S + n
                if n == 0:
                    after(dve, "dtx_done", b + km + 1)
                after(dve, "b_mm", 2 * b + i + 1)
                after(dve, "scan", 2 * (i - 1))
                nc.vector.tensor_tensor(dbx[:, n % 2], dtx[:, p], b_ps[:, n % 2].unsqueeze(1).broadcast_to([128, 2, CH]),
                                        ALU.mult).then_inc(dbx_done, 1)

            def run_scan(b, km, n, half):
                i = km * S + n
                after(dve, "dbx_done", i + 1)
                after(dve, "a_done", 2 * (2 * b + i) + half + 1)
                after(dve, "hc_done", i - S + 1)
                nc.vector.tensor_tensor_scan(h[:, n, half], d_a[:, n % DA, half], dbx[:, n % 2, half],
                                             carry[:, n, half:half + 1], ALU.mult, ALU.add).then_inc(scan, 1)

            def prelude(kp, p):
                den_bound(kp)
                den_reciprocal(kp)
                divide(kp, p)
                rest(kp)
                low_part(kp, p)
                rounding(kp)
                make_dt(kp, p)

            with dve.Fori(0, B) as b:
                fold(b)
                after(dve, "carried", b + b * NCH)
                nc.vector.memset(carry[:], 0.0).then_inc(carried, 1)
                prelude(b * SLOTS, 0)
                with dve.Fori(0, NCH // 2) as j:
                    for p in range(2):
                        km = b * NCH + 2 * j + p
                        kp = km + b + 1
                        o = 1 - p
                        steps = {
                            0: (lambda: den_bound(kp), None),
                            2: (lambda: skip(km, 0, o), lambda: skip(km, 1, o)),
                            3: (lambda: den_reciprocal(kp), lambda: divide(kp, o)),
                            8: (None, lambda: rest(kp)),
                            10: (None, lambda: low_part(kp, o)),
                            11: (None, lambda: rounding(kp)),
                            13: (None, lambda: make_dt(kp, o)),
                            15: (lambda: statistics(km), None),
                        }
                        weigh(b, km, 0, p)
                        after(dve, "carried", b + km + 1)
                        for n in range(S):
                            first, second = steps.get(n, (None, None))
                            if n + 1 < S:
                                weigh(b, km, n + 1, p)
                            if first:
                                first()
                            run_scan(b, km, n, 0)
                            if second:
                                second()
                            run_scan(b, km, n, 1)
                        after(dve, "scan", 2 * S * (km + 1))
                        nc.vector.tensor_copy(carry[:], h[:, :, :, CH - 1]).then_inc(carried, 1)
            skip(B * NCH, 0, 1)
            skip(B * NCH, 1, 1)
            statistics(B * NCH)


def phase_c(nc, t, gmat_dram, un_dram, o_dram, stats, out):
    with ExitStack() as ctx:
        def sb(name, shape, dt=F32):
            return ctx.enter_context(nc.sbuf_tensor(name, shape, dt))

        def sem(name):
            return ctx.enter_context(nc.semaphore(name))

        gn = sb("gn", [C, 2])
        share = sb("share", [C, C])
        eps = sb("gn_eps", [C, 1])
        moments = sb("moments", [C, B, 2])
        m2 = sb("m2", [C, B])
        g_mv = sb("g_mv", [C, B, 2])
        g_m2 = sb("g_m2", [C, B])
        g_std = sb("g_std", [C, B])
        scale = sb("scale", [C, B])
        shift = sb("shift", [C, B])
        ab = sb("ab", [C, 2, 2])
        gm = sb("gm_c", [KU, B, C])
        gm_b = sb("gm_b", [KU, 2, C])
        o_t = sb("o_t", [C, 2, CB])
        u_t = sb("u_c", [KU, 2, CB])
        act_t = sb("act_t", [C, 2, CB])
        r_t = sb("r_t", [C, 2, CB])
        res_ps = ctx.enter_context(nc.psum_tensor("res_ps", [C, 2, CB], F32))

        small_in = sem("C_small_in")
        step = sem("C_step")
        share_mm = sem("C_share_mm")
        rooted = sem("C_rooted")
        o_in = [sem(f"C_o_in{p}") for p in range(2)]
        u_in = [sem(f"C_u_in{p}") for p in range(2)]
        ab_done = sem("C_ab_done")
        gm_done = sem("C_gm_done")
        silu_done = sem("C_silu_done")
        res_mm = sem("C_res_mm")
        added = sem("C_added")
        stored = [sem(f"C_stored{p}") for p in range(2)]
        block = ctx.enter_context(nc.Block())

        @block.sync
        def _(sp):
            sp.dma_start(gn[:], t["gn"]).then_inc(small_in, 16)
            sp.dma_start(gm[:], gmat_dram.rearrange("b k c -> k b c")).then_inc(small_in, 16)
            sp.sem_inc(silu_done, 2)
            sp.sem_inc(res_mm, 2)
            for p in range(2):
                sp.sem_inc(stored[p], 16)
            with sp.Fori(0, B) as b:
                with sp.Fori(0, NCB // 2) as j:
                    for p in range(2):
                        k = b * NCB + 2 * j + p
                        c0 = (2 * j + p) * CB
                        sp.wait_ge(silu_done, k + 1)
                        sp.dma_start(o_t[:, p], o_dram[:, bass.ds((b * NCH + 1) * CH + c0, CB)]).then_inc(o_in[p], 16)
                        sp.wait_ge(res_mm, k + 1)
                        sp.dma_start(u_t[:, p], un_dram[:, bass.ds(b * SLOTS * CH + c0, CB)]).then_inc(u_in[p], 16)

        @block.scalar
        def _(act):
            act.wait_ge(step, STEPS_BEFORE_ROOT)
            nc.scalar.activation(g_std[:], g_m2[:], ACT.Sqrt, bias=eps[:]).then_inc(rooted, 1)
            with act.Fori(0, B) as b:
                act.wait_ge(ab_done, 2 * b + 2)
                with act.Fori(0, NCB // 2) as j:
                    for p in range(2):
                        k = b * NCB + 2 * j + p
                        act.wait_ge(o_in[p], 16 * (b * (NCB // 2) + j + 1))
                        act.wait_ge(added, k + 1)
                        nc.scalar.activation(act_t[:, p], o_t[:, p], ACT.Silu, bias=ab[:, 1, 0:1], scale=ab[:, 0, 0:1]
                                             ).then_inc(silu_done, 1)
                        act.wait_ge(added, k + 3)
                        act.dma_start(out[bass.ds(b, 1), :, bass.ds((2 * j + p) * CB, CB)]
                                      .rearrange("o c n -> (o c) n"), r_t[:, p]).then_inc(stored[p], 16)
            for p in range(2):
                act.wait_ge(stored[p], 16 * (B * NCB // 2 + 1))

        @block.tensor
        def _(pe):
            pe.wait_ge(step, STEPS_BEFORE_SHARE)
            nc.tensor.matmul(res_ps[:, 0, 0:2 * B], share[:], moments[:].rearrange("c b s -> c (b s)"),
                             start=True, stop=True).then_inc(share_mm, 1)
            pe.wait_ge(step, STEPS_BEFORE_ROOT)
            with pe.Fori(0, B) as b:
                with pe.Fori(0, NCB // 2) as j:
                    for p in range(2):
                        pe.wait_ge(gm_done, b + 1)
                        k = b * NCB + 2 * j + p
                        pe.wait_ge(u_in[p], 16 * (b * (NCB // 2) + j + 1))
                        pe.wait_ge(added, k + 1)
                        for i in range(CB // CH):
                            last = nc.tensor.matmul(res_ps[:, p, CH * i:CH * i + CH], gm_b[:, 0],
                                                    u_t[:, p, CH * i:CH * i + CH], start=True, stop=True)
                        last.then_inc(res_mm, 1)

        @block.vector
        def _(dve):
            done = [0]

            def chain(ins):
                done[0] += 1
                ins.then_inc(step, 1)
                dve.wait_ge(step, done[0])

            chain(nc.vector.memset(share[:], 0.0))
            for g in range(C // GROUP):
                s = slice(GROUP * g, GROUP * g + GROUP)
                chain(nc.vector.memset(share[s, s], 1.0 / GROUP))
            chain(nc.vector.memset(eps[:], GN_EPS))
            for b in range(B):
                chain(nc.vector.bn_aggr(moments[:, b], stats[:, b * NCH + 1:(b + 1) * NCH + 1, :]
                                        .rearrange("c k s -> c (k s)")))
            chain(nc.vector.tensor_tensor(m2[:], moments[:, :, 0], moments[:, :, 0], ALU.mult))
            chain(nc.vector.tensor_tensor(moments[:, :, 1], moments[:, :, 1], m2[:], ALU.add))
            assert done[0] == STEPS_BEFORE_SHARE
            dve.wait_ge(share_mm, 1)
            chain(nc.vector.tensor_copy(g_mv[:].rearrange("c b s -> c (b s)"), res_ps[:, 0, 0:2 * B]))
            chain(nc.vector.tensor_tensor(m2[:], g_mv[:, :, 0], g_mv[:, :, 0], ALU.mult))
            chain(nc.vector.tensor_tensor(g_m2[:], g_mv[:, :, 1], m2[:], ALU.subtract))
            assert done[0] == STEPS_BEFORE_ROOT
            dve.wait_ge(rooted, 1)
            dve.wait_ge(small_in, 32)
            chain(nc.vector.reciprocal(m2[:], g_std[:]))
            chain(nc.vector.tensor_scalar(scale[:], m2[:], gn[:, 0:1], None, ALU.mult))
            chain(nc.vector.tensor_tensor(m2[:], g_mv[:, :, 0], scale[:], ALU.mult))
            chain(nc.vector.tensor_scalar(shift[:], m2[:], -1.0, gn[:, 1:2], ALU.mult, ALU.add))
            dve.sem_inc(added, 2)
            with dve.Fori(0, B) as b:
                dve.wait_ge(silu_done, b * NCB + 2)
                dve.wait_ge(res_mm, b * NCB + 2)
                nc.vector.tensor_copy(ab[:, 0, 0:1], scale[:, bass.ds(b, 1)]).then_inc(ab_done, 1)
                nc.vector.tensor_copy(ab[:, 1, 0:1], shift[:, bass.ds(b, 1)]).then_inc(ab_done, 1)
                nc.vector.tensor_copy(gm_b[:, 0], gm[:, bass.ds(b, 1), :].rearrange("k o c -> k (o c)")
                                      ).then_inc(gm_done, 1)
                with dve.Fori(0, NCB // 2) as j:
                    for p in range(2):
                        k = b * NCB + 2 * j + p
                        dve.wait_ge(silu_done, k + 3)
                        dve.wait_ge(res_mm, k + 3)
                        dve.wait_ge(stored[p], 16 * (b * (NCB // 2) + j + 1))
                        nc.vector.tensor_tensor(r_t[:, p], act_t[:, p], res_ps[:, p], ALU.add).then_inc(added, 1)


STEPS_BEFORE_SHARE = 1 + C // GROUP + 1 + B + 2
STEPS_BEFORE_ROOT = STEPS_BEFORE_SHARE + 3


def build(nc, t, out):
    uq = nc.dram_tensor("uq", (KU, (B * SLOTS + 1) * CH), F32, kind="Internal").ap()
    un_dram = nc.dram_tensor("un_dram", (KU, B * SLOTS * CH), F32, kind="Internal").ap()
    o_dram = nc.dram_tensor("o_dram", (C, (B * NCH + 1) * CH), F32, kind="Internal").ap()
    mat_dram = nc.dram_tensor("mat_dram", (B, KU, C + 1), F32, kind="Internal").ap()
    gmat_dram = nc.dram_tensor("gmat_dram", (B, KU, C), F32, kind="Internal").ap()
    phase_a(nc, t, uq, mat_dram)
    with nc.sbuf_tensor("stats", [C, B * NCH + 1, 6], F32) as stats:
        phase_b(nc, t, uq, mat_dram, gmat_dram, un_dram, o_dram, stats)
        phase_c(nc, t, gmat_dram, un_dram, o_dram, stats, out)


def kernel(x, **w):
    import numpy as np
    import concourse.bacc as bacc
    from concourse.bass_utils import run_bass_kernel_spmd

    l0 = {k[8:]: np.asarray(v) for k, v in w.items() if k.startswith("L0_conv_")}
    l1 = {k[8:]: np.asarray(v) for k, v in w.items() if k.startswith("L1_conv_")}
    dil = [l0["w2"], l0["w3"], l0["w4"]]
    at = [(dy + 1, dx + 1) for dy, dx in TAPS]
    arrays = {
        "x": np.asarray(x),
        "w_center": np.concatenate([l0["w1"][:, :, 0, 0]] + [v[:, :, 1, 1] for v in dil]).T,
        "w_taps": np.stack([np.stack([v[:, :, i, j].T for i, j in at], 1) for v in dil], 1),
        "w_kv": np.concatenate([l0["wk"][:, :, 0, 0], l0["wv"][:, :, 0, 0]]).T,
        "b_kv": np.concatenate([l0["bk"], l0["bv"]]),
        "w_q": l0["wq"][:, :, 0, 0].T,
        "b_q": l0["bq"][:, None],
        "bn": np.stack([l0["bn_scale"].ravel(), l0["bn_bias"].ravel(), l0["bn_mean"].ravel(),
                        l0["bn_var"].ravel()], 1),
        "gamma": l0["gamma"],
        "w_in": l1["W_in"],
        "conv_w": l1["conv_w"].T,
        "conv_b": l1["conv_b"].reshape(2, 128).T,
        "w_x": l1["W_x"].reshape(2, 128, R + 2 * S).transpose(1, 0, 2),
        "w_dt": l1["W_dt"],
        "b_dt": l1["b_dt"].reshape(2, 128).T,
        "a_log": l1["A_log"].reshape(2, 128, S).transpose(1, 0, 2),
        "d_skip": l1["D"].reshape(2, 128).T,
        "w_out": l1["W_out"].reshape(2, 128, C).transpose(1, 0, 2),
        "gn": np.stack([l1["gn_gamma"], l1["gn_beta"]], 1),
    }
    arrays = {k: np.ascontiguousarray(v) for k, v in arrays.items()}
    nc = bacc.Bacc("TRN2", target_bir_lowering=False, num_devices=1)
    t = {k: nc.dram_tensor("in_" + k, v.shape, F32, kind="ExternalInput").ap() for k, v in arrays.items()}
    out = nc.dram_tensor("out", (B, C, N), F32, kind="ExternalOutput").ap()
    build(nc, t, out)
    r = run_bass_kernel_spmd(nc, [{"in_" + k: v for k, v in arrays.items()}], core_ids=[0])
    return r.results[0]["out"].reshape(B, C, H, W)
```
